# Optimizing a Trainium2 kernel written in Bass

```python
import numpy as np
import jax
import jax.numpy as jnp

def _softmax(x, axis=-1):
    return jax.nn.softmax(x, axis=axis)

def _gelu(x):
    return jax.nn.gelu(x, approximate=True)

def _silu(x):
    return jax.nn.silu(x)

def _sigmoid(x):
    return jax.nn.sigmoid(x)

def _layernorm(x, axis=-1, eps=1e-05):
    m = jnp.mean(x, axis=axis, keepdims=True)
    v = jnp.var(x, axis=axis, keepdims=True)
    return (x - m) / jnp.sqrt(v + eps)

def _scatter_add(tgt, idx, src, axis=0):
    return tgt.at[idx].add(src)

def _segment_sum(src, seg, n):
    return jax.ops.segment_sum(src, seg, n)
kernel_name = 'mk_perceiver_d4_seqx_r4_e897bb'

def setup_inputs(seed: int=0):
    np.random.seed(seed)
    _w = jnp.asarray

    def _rec_inputs():
        import jax
        import jax.numpy as jnp
        _rk = jax.random.key(seed)
        x = -0.0002928 + 1 * jax.random.normal(jax.random.fold_in(_rk, 1), (64, 32, 256), jnp.float32)
        _lenS = 32 - jax.random.randint(jax.random.fold_in(_rk, 7), (64,), 0, max(1, 32 // 4) + 1, jnp.int32)
        _lenS2 = 257 - jax.random.randint(jax.random.fold_in(_rk, 8), (64,), 0, max(1, 257 // 4) + 1, jnp.int32)
        _ctx_1024P = jax.random.normal(jax.random.fold_in(_rk, 11), (64, 16, 256), jnp.float32)
        _ctx_1024c = jax.random.dirichlet(jax.random.fold_in(_rk, 511), 0.3 * jnp.ones((16,), jnp.float32), (64, 257))
        _ctx_1024t = jnp.einsum('bsk,bkd->bsd', _ctx_1024c, _ctx_1024P)
        _ctx_1024t = _ctx_1024t * jax.lax.rsqrt(jnp.mean(jnp.square(_ctx_1024t)) + 1e-12) * 0.953939
        ctx_1024 = 2.81802e-05 + 1.00001 * (_ctx_1024t + 0.3 * jax.random.normal(jax.random.fold_in(_rk, 611), (64, 257, 256), jnp.float32))
        _validS = jnp.arange(32)[None, :] < _lenS[:, None]
        _validS2 = jnp.arange(257)[None, :] < _lenS2[:, None]
        _causal = jnp.tril(jnp.ones((32, 32), dtype=bool))
        mask_BxS2_bk0 = jnp.logical_not(jnp.broadcast_to(_validS2[:, :], (64, 257)))
        return (x, ctx_1024, mask_BxS2_bk0)
    x, ctx_1024, mask_BxS2_bk0 = _rec_inputs()

    def _L0_xattn_setup():
        import jax, jax.numpy as jnp
        import numpy as np
        NUM_HEADS, NUM_KV, HEAD_DIM, WIDTH = (4, 1, 64, 256)
        MASK_FILL = -2.3819763e+38

        def _apply_rope(x, positions, max_wavelength=10000.0):
            d = x.shape[-1]
            freq_exp = 2.0 / d * jnp.arange(d // 2, dtype=jnp.float32)
            timescale = max_wavelength ** freq_exp
            radians = positions[..., None].astype(jnp.float32) / timescale
            radians = radians[..., None, :]
            sin, cos = (jnp.sin(radians), jnp.cos(radians))
            x1, x2 = jnp.split(x, 2, axis=-1)
            out = jnp.concatenate([x1 * cos - x2 * sin, x2 * cos + x1 * sin], axis=-1)
            return out.astype(x.dtype)

        def _rmsnorm(x, scale):
            var = jnp.mean(jnp.square(x.astype(jnp.float32)), axis=-1, keepdims=True)
            normed = x * jax.lax.rsqrt(var + 1e-06)
            return (normed * (1 + scale)).astype(x.dtype)
        key = jax.random.key(seed)
        ks = jax.random.split(key, 7)
        B, T, S = (8, 128, 512)
        return {'x': jax.random.normal(ks[0], (B, T, WIDTH), jnp.float32), 'mem_seq': jax.random.normal(ks[1], (B, S, WIDTH), jnp.float32), 'mem_mask': jax.random.randint(ks[2], (B, S), 0, 2).astype(bool), 'rms_scale': jax.random.normal(ks[3], (WIDTH,), jnp.float32) * 0.02, 'q_w': jax.random.normal(ks[4], (NUM_HEADS, WIDTH, HEAD_DIM), jnp.float32) / np.sqrt(WIDTH), 'kv_w': jax.random.normal(ks[5], (2, NUM_KV, WIDTH, HEAD_DIM), jnp.float32) / np.sqrt(WIDTH), 'out_w': jax.random.normal(ks[6], (NUM_HEADS, HEAD_DIM, WIDTH), jnp.float32) / np.sqrt(NUM_HEADS * HEAD_DIM)}
    _L0_xattn_all = _L0_xattn_setup()
    _L0_xattn_in = {k: v for k, v in _L0_xattn_all.items() if k in ('rms_scale', 'q_w', 'kv_w', 'out_w')}
    del _L0_xattn_all

    def _L0_attn_setup():
        import jax, jax.numpy as jnp
        import numpy as np
        NUM_HEADS = 16
        EPS = float(jnp.finfo(jnp.float32).eps)

        def rms_norm(x, w):
            ms = jnp.mean(x * x, axis=-1, keepdims=True)
            return x * jax.lax.rsqrt(ms + EPS) * w
        key = jax.random.key(seed)
        k = jax.random.split(key, 5)
        B, N, D = (4, 512, 256)
        Dh = D // NUM_HEADS
        return {'x': jax.random.normal(k[0], (B, N, D), dtype=jnp.float32), 'Wq': jax.random.normal(k[1], (D, D), dtype=jnp.float32) * 0.02, 'Wk': jax.random.normal(k[2], (D, D), dtype=jnp.float32) * 0.02, 'Wv': jax.random.normal(k[3], (D, D), dtype=jnp.float32) * 0.02, 'Wo': jax.random.normal(k[4], (D, D), dtype=jnp.float32) * 0.02, 'qn_w': jnp.ones((Dh,), dtype=jnp.float32), 'kn_w': jnp.ones((Dh,), dtype=jnp.float32)}
    _L0_attn_all = _L0_attn_setup()
    _L0_attn_in = {k: v for k, v in _L0_attn_all.items() if k in ('Wq', 'Wk', 'Wv', 'Wo', 'qn_w', 'kn_w')}
    del _L0_attn_all

    def _L0_ffn_setup():
        import jax, jax.numpy as jnp
        import numpy as np
        key = jax.random.key(seed)
        k0, k1, k2, k3 = jax.random.split(key, 4)
        B, S, D, F, E = (8, 512, 256, 512, 8)
        x = jax.random.normal(k0, (B, S, D), dtype=jnp.float32)
        Wg = jax.random.normal(k1, (D, E), dtype=jnp.float32) * 0.02
        W1 = jax.random.normal(k2, (E, D, F), dtype=jnp.float32) * 0.02
        W2 = jax.random.normal(k3, (E, F, D), dtype=jnp.float32) * 0.02
        return {'x': x, 'Wg': Wg, 'W1': W1, 'W2': W2}
    _L0_ffn_all = _L0_ffn_setup()
    _L0_ffn_in = {k: v for k, v in _L0_ffn_all.items() if k in ('Wg', 'W1', 'W2')}
    del _L0_ffn_all

    def _L1_xattn_setup():
        import jax, jax.numpy as jnp
        import numpy as np
        H = 256
        B = 8
        L_CHAR = 512
        L_SUB = 256

        def _linear(x, W, b):
            return jnp.einsum('blh,oh->blo', x, W) + b

        def _interp_linear(x, out_len):
            L_in = x.shape[1]
            pos = (jnp.arange(out_len, dtype=x.dtype) + 0.5) * (L_in / out_len) - 0.5
            pos = jnp.clip(pos, 0.0, L_in - 1)
            lo = jnp.floor(pos).astype(jnp.int32)
            hi = jnp.minimum(lo + 1, L_in - 1)
            w = (pos - lo.astype(x.dtype))[None, :, None]
            return x[:, lo] * (1 - w) + x[:, hi] * w
        key = jax.random.key(seed)
        ks = jax.random.split(key, 18)
        s = 0.02
        inp = {'char_emb': jax.random.normal(ks[0], (B, L_CHAR, H), jnp.float32), 'subword_emb': jax.random.normal(ks[1], (B, L_SUB, H), jnp.float32)}
        names = ['Wq_c', 'Wk_s', 'Wv_s', 'Wq_s', 'Wk_c', 'Wv_c']
        for i, n in enumerate(names):
            inp[n] = jax.random.normal(ks[2 + 2 * i], (H, H), jnp.float32) * s
            inp['b' + n[1:]] = jax.random.normal(ks[3 + 2 * i], (H,), jnp.float32) * s
        inp['Wg'] = jax.random.normal(ks[14], (H, 2 * H), jnp.float32) * s
        inp['bg'] = jax.random.normal(ks[15], (H,), jnp.float32) * s
        return inp
    _L1_xattn_all = _L1_xattn_setup()
    _L1_xattn_in = {k: v for k, v in _L1_xattn_all.items() if k in ('Wq_c', 'bq_c', 'Wk_s', 'bk_s', 'Wv_s', 'bv_s', 'Wq_s', 'bq_s', 'Wk_c', 'bk_c', 'Wv_c', 'bv_c', 'Wg', 'bg')}
    del _L1_xattn_all

    def _L1_attn_setup():
        import jax, jax.numpy as jnp
        import numpy as np
        import math
        N_HEADS, D_HEAD, D_MODEL = (16, 64, 256)
        B, S = (4, 512)
        NEG_MASK = -100000.0
        key = jax.random.key(seed)
        ks = jax.random.split(key, 9)
        bound = math.sqrt(6.0 / (D_MODEL + D_HEAD))

        def w(k):
            return jax.random.uniform(k, (N_HEADS, D_MODEL, D_HEAD), jnp.float32, -bound, bound)
        return {'x': jax.random.normal(ks[0], (B, S, D_MODEL), jnp.float32), 'Q_w': w(ks[1]), 'Q_b': jnp.zeros((N_HEADS, D_HEAD), jnp.float32), 'K_w': w(ks[2]), 'K_b': jnp.zeros((N_HEADS, D_HEAD), jnp.float32), 'V_w': w(ks[3]), 'V_b': jnp.zeros((N_HEADS, D_HEAD), jnp.float32), 'O_w': jax.random.uniform(ks[4], (N_HEADS, D_HEAD, D_MODEL), jnp.float32, -bound, bound), 'O_b': jnp.zeros((D_MODEL,), jnp.float32)}
    _L1_attn_all = _L1_attn_setup()
    _L1_attn_in = {k: v for k, v in _L1_attn_all.items() if k in ('Q_w', 'Q_b', 'K_w', 'K_b', 'V_w', 'V_b', 'O_w', 'O_b')}
    del _L1_attn_all

    def _L1_ffn_setup():
        import jax, jax.numpy as jnp
        import numpy as np
        B, S, H = (4, 512, 256)
        E = 8
        GS = 2
        NG = E // GS
        F = int(H * 4 * (2.0 / 3.0))
        key = jax.random.key(seed)
        ks = jax.random.split(key, 7)
        sc_h = 1.0 / np.sqrt(H)
        sc_f = 1.0 / np.sqrt(F)
        return {'x': jax.random.normal(ks[0], (B, S, H), dtype=jnp.float32), 'Wr': jax.random.normal(ks[1], (H, E), dtype=jnp.float32) * sc_h, 'br': jnp.zeros((E,), dtype=jnp.float32), 'W_up': jax.random.normal(ks[2], (NG, H, F), dtype=jnp.float32) * sc_h, 'b_up': jax.random.normal(ks[3], (NG, F), dtype=jnp.float32) * 0.01, 'W_down': jax.random.normal(ks[4], (E, F, H), dtype=jnp.float32) * sc_f, 'b_down': jax.random.normal(ks[5], (E, H), dtype=jnp.float32) * 0.01}
    _L1_ffn_all = _L1_ffn_setup()
    _L1_ffn_in = {k: v for k, v in _L1_ffn_all.items() if k in ('Wr', 'br', 'W_up', 'b_up', 'W_down', 'b_down')}
    del _L1_ffn_all

    def _L2_xattn_setup():
        import jax, jax.numpy as jnp
        import numpy as np
        EPS = 1e-05

        def layernorm(x, g, b):
            mu = jnp.mean(x, axis=-1, keepdims=True)
            var = jnp.var(x, axis=-1, keepdims=True)
            return (x - mu) * jax.lax.rsqrt(var + EPS) * g + b
        DIM = 256
        CTX = 256
        HEADS = 12
        DHEAD = 64
        INNER = HEADS * DHEAD
        B = 4
        F = 512
        J = 256
        key = jax.random.key(seed)
        ks = jax.random.split(key, 8)
        s = lambda d: 1.0 / np.sqrt(d)
        return {'x': jax.random.normal(ks[0], (B, F, DIM), jnp.float32), 'tab_x': jax.random.normal(ks[1], (B, J, CTX), jnp.float32), 'tab_g': jnp.ones((CTX,), jnp.float32), 'tab_b': jnp.zeros((CTX,), jnp.float32), 'vid_g': jnp.ones((DIM,), jnp.float32), 'vid_b': jnp.zeros((DIM,), jnp.float32), 'Wq': jax.random.normal(ks[2], (DIM, INNER), jnp.float32) * s(DIM), 'Wk': jax.random.normal(ks[3], (CTX, INNER), jnp.float32) * s(CTX), 'Wv': jax.random.normal(ks[4], (CTX, INNER), jnp.float32) * s(CTX), 'q_g': jnp.ones((INNER,), jnp.float32), 'q_b': jnp.zeros((INNER,), jnp.float32), 'k_g': jnp.ones((INNER,), jnp.float32), 'k_b': jnp.zeros((INNER,), jnp.float32), 'Wo': jax.random.normal(ks[5], (INNER, DIM), jnp.float32) * s(INNER), 'bo': jnp.zeros((DIM,), jnp.float32)}
    _L2_xattn_all = _L2_xattn_setup()
    _L2_xattn_in = {k: v for k, v in _L2_xattn_all.items() if k in ('tab_g', 'tab_b', 'vid_g', 'vid_b', 'Wq', 'Wk', 'Wv', 'q_g', 'q_b', 'k_g', 'k_b', 'Wo', 'bo')}
    del _L2_xattn_all

    def _L2_attn_setup():
        import jax, jax.numpy as jnp
        import numpy as np
        import math
        B, N, DIM, H, DH, NNULL = (2, 512, 256, 16, 64, 2)
        SCALE = 8.0
        LN_EPS = 1e-05

        def _alibi_slopes(heads):
            start = 2.0 ** (-2.0 ** (-(math.log2(heads) - 3)))
            return np.array([start * start ** i for i in range(heads)], dtype=np.float32)

        def _l2norm(t):
            n = jnp.sqrt(jnp.sum(t * t, axis=-1, keepdims=True))
            return t / jnp.maximum(n, 1e-12)
        key = jax.random.key(seed)
        ks = jax.random.split(key, 6)
        inner = H * DH
        return {'x': jax.random.normal(ks[0], (B, N, DIM), dtype=jnp.float32), 'norm_g': jnp.ones((DIM,), jnp.float32), 'norm_b': jnp.zeros((DIM,), jnp.float32), 'Wq': jax.random.normal(ks[1], (DIM, inner), jnp.float32) * 0.02, 'Wkv': jax.random.normal(ks[2], (DIM, 2 * inner), jnp.float32) * 0.02, 'q_scale': jnp.ones((DH,), jnp.float32), 'k_scale': jnp.ones((DH,), jnp.float32), 'null_kv': jax.random.normal(ks[3], (H, 2 * NNULL, DH), jnp.float32), 'Wout': jax.random.normal(ks[4], (inner, DIM), jnp.float32) * 0.02}
    _L2_attn_all = _L2_attn_setup()
    _L2_attn_in = {k: v for k, v in _L2_attn_all.items() if k in ('norm_g', 'norm_b', 'Wq', 'Wkv', 'q_scale', 'k_scale', 'null_kv', 'Wout')}
    del _L2_attn_all

    def _L2_ffn_setup():
        import jax, jax.numpy as jnp
        import numpy as np
        D_IN, D_HID = (256, 1024)

        def _ternary(key, shape):
            return jax.random.randint(key, shape, -1, 2).astype(jnp.float32)

        def _tlin(x, w, s):
            return jnp.einsum('bsi,oi->bso', x, w) * s
        key = jax.random.key(seed)
        ks = jax.random.split(key, 12)
        inv = lambda fan: 1.0 / np.sqrt(fan).astype(np.float32)
        return {'x': jax.random.normal(ks[0], (4, 512, D_IN), dtype=jnp.float32), 'w1_w': _ternary(ks[1], (D_HID, D_IN)), 'w1_s': jax.random.uniform(ks[2], (D_HID,), dtype=jnp.float32) * inv(D_IN), 'w2_w': _ternary(ks[3], (D_HID, D_IN)), 'w2_s': jax.random.uniform(ks[4], (D_HID,), dtype=jnp.float32) * inv(D_IN), 'h1_w': _ternary(ks[5], (D_HID, D_HID)), 'h1_s': jax.random.uniform(ks[6], (D_HID,), dtype=jnp.float32) * inv(D_HID), 'h2_w': _ternary(ks[7], (D_HID, D_HID)), 'h2_s': jax.random.uniform(ks[8], (D_HID,), dtype=jnp.float32) * inv(D_HID), 'w3_w': _ternary(ks[9], (D_IN, D_HID)), 'w3_s': jax.random.uniform(ks[10], (D_IN,), dtype=jnp.float32) * inv(D_HID)}
    _L2_ffn_all = _L2_ffn_setup()
    _L2_ffn_in = {k: v for k, v in _L2_ffn_all.items() if k in ('w1_w', 'w1_s', 'w2_w', 'w2_s', 'h1_w', 'h1_s', 'h2_w', 'h2_s', 'w3_w', 'w3_s')}
    del _L2_ffn_all

    def _L3_xattn_setup():
        import jax, jax.numpy as jnp
        import numpy as np
        D_MODEL = 256
        N_HEAD = 16
        D_K = D_MODEL // N_HEAD

        def _split_heads(x):
            B, S, _ = x.shape
            return x.reshape(B, S, N_HEAD, D_K).transpose(0, 2, 1, 3)
        key = jax.random.key(seed)
        ks = jax.random.split(key, 11)
        B, S = (2, 512)
        scale = 1.0 / np.sqrt(D_MODEL)
        inp = {'q': jax.random.normal(ks[0], (B, S, D_MODEL), jnp.float32), 'k': jax.random.normal(ks[1], (B, S, D_MODEL), jnp.float32), 'v': jax.random.normal(ks[2], (B, S, D_MODEL), jnp.float32), 'Wq': jax.random.normal(ks[3], (D_MODEL, D_MODEL), jnp.float32) * scale, 'bq': jnp.zeros((D_MODEL,), jnp.float32), 'Wk': jax.random.normal(ks[4], (D_MODEL, D_MODEL), jnp.float32) * scale, 'bk': jnp.zeros((D_MODEL,), jnp.float32), 'Wv': jax.random.normal(ks[5], (D_MODEL, D_MODEL), jnp.float32) * scale, 'bv': jnp.zeros((D_MODEL,), jnp.float32), 'Wo': jax.random.normal(ks[6], (D_MODEL, D_MODEL), jnp.float32) * scale, 'bo': jnp.zeros((D_MODEL,), jnp.float32)}
        return inp
    _L3_xattn_all = _L3_xattn_setup()
    _L3_xattn_in = {k: v for k, v in _L3_xattn_all.items() if k in ('Wq', 'bq', 'Wk', 'bk', 'Wv', 'bv', 'Wo', 'bo')}
    del _L3_xattn_all

    def _L3_attn_setup():
        import jax, jax.numpy as jnp
        import numpy as np
        DIM = 256
        HEADS = 16
        DIM_HEAD = 64
        INNER = HEADS * DIM_HEAD
        EPS = 1e-10

        def safe_softmax(s):
            m = jnp.max(s, axis=-1, keepdims=True)
            e = jnp.exp(s - m)
            return e / (jnp.sum(e, axis=-1, keepdims=True) + EPS)
        key = jax.random.key(seed)
        ks = jax.random.split(key, 6)
        B, N = (4, 512)
        x = jax.random.normal(ks[0], (B, N, DIM), dtype=jnp.float32)
        s_in = 1.0 / np.sqrt(DIM)
        s_inner = 1.0 / np.sqrt(INNER)
        Wq = jax.random.uniform(ks[1], (INNER, DIM), jnp.float32, -s_in, s_in)
        Wk = jax.random.uniform(ks[2], (INNER, DIM), jnp.float32, -s_in, s_in)
        Wv = jax.random.uniform(ks[3], (INNER, DIM), jnp.float32, -s_in, s_in)
        Wo = jax.random.uniform(ks[4], (DIM, INNER), jnp.float32, -s_inner, s_inner)
        bo = jax.random.uniform(ks[5], (DIM,), jnp.float32, -s_inner, s_inner)
        return {'x': x, 'Wq': Wq, 'Wk': Wk, 'Wv': Wv, 'Wo': Wo, 'bo': bo}
    _L3_attn_all = _L3_attn_setup()
    _L3_attn_in = {k: v for k, v in _L3_attn_all.items() if k in ('Wq', 'Wk', 'Wv', 'Wo', 'bo')}
    del _L3_attn_all

    def _L3_ffn_setup():
        import jax, jax.numpy as jnp
        import numpy as np
        IN_F = 256
        OUT_F = 256
        B, S = (8, 1024)

        def _pack_ternary(tern):
            enc = (tern + 1.0).astype(jnp.int32).reshape(-1)
            return (enc[0::4] | enc[1::4] << 2 | enc[2::4] << 4 | enc[3::4] << 6).astype(jnp.int32)
        key = jax.random.key(seed)
        kx, kw = jax.random.split(key)
        x = jax.random.normal(kx, (B, S, IN_F), dtype=jnp.float32)
        w = jax.random.normal(kw, (OUT_F, IN_F), dtype=jnp.float32) * 0.02
        scale = jnp.maximum(jnp.mean(jnp.abs(w)), 1e-05)
        wn = w / scale
        tern = jnp.sign(wn) * (jnp.abs(wn) > 0.5).astype(jnp.float32)
        packed = _pack_ternary(tern)
        bias = jnp.zeros((OUT_F,), dtype=jnp.float32)
        return {'x': x, 'packed_weight': packed, 'weight_scale': scale.reshape(1), 'bias': bias}
    _L3_ffn_all = _L3_ffn_setup()
    _L3_ffn_in = {k: v for k, v in _L3_ffn_all.items() if k in ('packed_weight', 'weight_scale', 'bias')}
    del _L3_ffn_all
    return {'x': x, 'ctx_1024': ctx_1024, 'mask_BxS2_bk0': mask_BxS2_bk0, 'L0_xattn_rms_scale': _L0_xattn_in['rms_scale'], 'L0_xattn_q_w': _L0_xattn_in['q_w'], 'L0_xattn_kv_w': _L0_xattn_in['kv_w'], 'L0_xattn_out_w': _L0_xattn_in['out_w'], 'L0_attn_Wq': _L0_attn_in['Wq'], 'L0_attn_Wk': _L0_attn_in['Wk'], 'L0_attn_Wv': _L0_attn_in['Wv'], 'L0_attn_Wo': _L0_attn_in['Wo'], 'L0_attn_qn_w': _L0_attn_in['qn_w'], 'L0_attn_kn_w': _L0_attn_in['kn_w'], 'L0_ffn_Wg': _L0_ffn_in['Wg'], 'L0_ffn_W1': _L0_ffn_in['W1'], 'L0_ffn_W2': _L0_ffn_in['W2'], 'L1_xattn_Wq_c': _L1_xattn_in['Wq_c'], 'L1_xattn_bq_c': _L1_xattn_in['bq_c'], 'L1_xattn_Wk_s': _L1_xattn_in['Wk_s'], 'L1_xattn_bk_s': _L1_xattn_in['bk_s'], 'L1_xattn_Wv_s': _L1_xattn_in['Wv_s'], 'L1_xattn_bv_s': _L1_xattn_in['bv_s'], 'L1_xattn_Wq_s': _L1_xattn_in['Wq_s'], 'L1_xattn_bq_s': _L1_xattn_in['bq_s'], 'L1_xattn_Wk_c': _L1_xattn_in['Wk_c'], 'L1_xattn_bk_c': _L1_xattn_in['bk_c'], 'L1_xattn_Wv_c': _L1_xattn_in['Wv_c'], 'L1_xattn_bv_c': _L1_xattn_in['bv_c'], 'L1_xattn_Wg': _L1_xattn_in['Wg'], 'L1_xattn_bg': _L1_xattn_in['bg'], 'L1_attn_Q_w': _L1_attn_in['Q_w'], 'L1_attn_Q_b': _L1_attn_in['Q_b'], 'L1_attn_K_w': _L1_attn_in['K_w'], 'L1_attn_K_b': _L1_attn_in['K_b'], 'L1_attn_V_w': _L1_attn_in['V_w'], 'L1_attn_V_b': _L1_attn_in['V_b'], 'L1_attn_O_w': _L1_attn_in['O_w'], 'L1_attn_O_b': _L1_attn_in['O_b'], 'L1_ffn_Wr': _L1_ffn_in['Wr'], 'L1_ffn_br': _L1_ffn_in['br'], 'L1_ffn_W_up': _L1_ffn_in['W_up'], 'L1_ffn_b_up': _L1_ffn_in['b_up'], 'L1_ffn_W_down': _L1_ffn_in['W_down'], 'L1_ffn_b_down': _L1_ffn_in['b_down'], 'L2_xattn_tab_g': _L2_xattn_in['tab_g'], 'L2_xattn_tab_b': _L2_xattn_in['tab_b'], 'L2_xattn_vid_g': _L2_xattn_in['vid_g'], 'L2_xattn_vid_b': _L2_xattn_in['vid_b'], 'L2_xattn_Wq': _L2_xattn_in['Wq'], 'L2_xattn_Wk': _L2_xattn_in['Wk'], 'L2_xattn_Wv': _L2_xattn_in['Wv'], 'L2_xattn_q_g': _L2_xattn_in['q_g'], 'L2_xattn_q_b': _L2_xattn_in['q_b'], 'L2_xattn_k_g': _L2_xattn_in['k_g'], 'L2_xattn_k_b': _L2_xattn_in['k_b'], 'L2_xattn_Wo': _L2_xattn_in['Wo'], 'L2_xattn_bo': _L2_xattn_in['bo'], 'L2_attn_norm_g': _L2_attn_in['norm_g'], 'L2_attn_norm_b': _L2_attn_in['norm_b'], 'L2_attn_Wq': _L2_attn_in['Wq'], 'L2_attn_Wkv': _L2_attn_in['Wkv'], 'L2_attn_q_scale': _L2_attn_in['q_scale'], 'L2_attn_k_scale': _L2_attn_in['k_scale'], 'L2_attn_null_kv': _L2_attn_in['null_kv'], 'L2_attn_Wout': _L2_attn_in['Wout'], 'L2_ffn_w1_w': _L2_ffn_in['w1_w'], 'L2_ffn_w1_s': _L2_ffn_in['w1_s'], 'L2_ffn_w2_w': _L2_ffn_in['w2_w'], 'L2_ffn_w2_s': _L2_ffn_in['w2_s'], 'L2_ffn_h1_w': _L2_ffn_in['h1_w'], 'L2_ffn_h1_s': _L2_ffn_in['h1_s'], 'L2_ffn_h2_w': _L2_ffn_in['h2_w'], 'L2_ffn_h2_s': _L2_ffn_in['h2_s'], 'L2_ffn_w3_w': _L2_ffn_in['w3_w'], 'L2_ffn_w3_s': _L2_ffn_in['w3_s'], 'L3_xattn_Wq': _L3_xattn_in['Wq'], 'L3_xattn_bq': _L3_xattn_in['bq'], 'L3_xattn_Wk': _L3_xattn_in['Wk'], 'L3_xattn_bk': _L3_xattn_in['bk'], 'L3_xattn_Wv': _L3_xattn_in['Wv'], 'L3_xattn_bv': _L3_xattn_in['bv'], 'L3_xattn_Wo': _L3_xattn_in['Wo'], 'L3_xattn_bo': _L3_xattn_in['bo'], 'L3_attn_Wq': _L3_attn_in['Wq'], 'L3_attn_Wk': _L3_attn_in['Wk'], 'L3_attn_Wv': _L3_attn_in['Wv'], 'L3_attn_Wo': _L3_attn_in['Wo'], 'L3_attn_bo': _L3_attn_in['bo'], 'L3_ffn_packed_weight': _L3_ffn_in['packed_weight'], 'L3_ffn_weight_scale': _L3_ffn_in['weight_scale'], 'L3_ffn_bias': _L3_ffn_in['bias']}

def reference(x, ctx_1024, mask_BxS2_bk0, L0_xattn_rms_scale, L0_xattn_q_w, L0_xattn_kv_w, L0_xattn_out_w, L0_attn_Wq, L0_attn_Wk, L0_attn_Wv, L0_attn_Wo, L0_attn_qn_w, L0_attn_kn_w, L0_ffn_Wg, L0_ffn_W1, L0_ffn_W2, L1_xattn_Wq_c, L1_xattn_bq_c, L1_xattn_Wk_s, L1_xattn_bk_s, L1_xattn_Wv_s, L1_xattn_bv_s, L1_xattn_Wq_s, L1_xattn_bq_s, L1_xattn_Wk_c, L1_xattn_bk_c, L1_xattn_Wv_c, L1_xattn_bv_c, L1_xattn_Wg, L1_xattn_bg, L1_attn_Q_w, L1_attn_Q_b, L1_attn_K_w, L1_attn_K_b, L1_attn_V_w, L1_attn_V_b, L1_attn_O_w, L1_attn_O_b, L1_ffn_Wr, L1_ffn_br, L1_ffn_W_up, L1_ffn_b_up, L1_ffn_W_down, L1_ffn_b_down, L2_xattn_tab_g, L2_xattn_tab_b, L2_xattn_vid_g, L2_xattn_vid_b, L2_xattn_Wq, L2_xattn_Wk, L2_xattn_Wv, L2_xattn_q_g, L2_xattn_q_b, L2_xattn_k_g, L2_xattn_k_b, L2_xattn_Wo, L2_xattn_bo, L2_attn_norm_g, L2_attn_norm_b, L2_attn_Wq, L2_attn_Wkv, L2_attn_q_scale, L2_attn_k_scale, L2_attn_null_kv, L2_attn_Wout, L2_ffn_w1_w, L2_ffn_w1_s, L2_ffn_w2_w, L2_ffn_w2_s, L2_ffn_h1_w, L2_ffn_h1_s, L2_ffn_h2_w, L2_ffn_h2_s, L2_ffn_w3_w, L2_ffn_w3_s, L3_xattn_Wq, L3_xattn_bq, L3_xattn_Wk, L3_xattn_bk, L3_xattn_Wv, L3_xattn_bv, L3_xattn_Wo, L3_xattn_bo, L3_attn_Wq, L3_attn_Wk, L3_attn_Wv, L3_attn_Wo, L3_attn_bo, L3_ffn_packed_weight, L3_ffn_weight_scale, L3_ffn_bias):
    import jax
    import jax.numpy as jnp

    def _L0_xattn_ref(x, mem_seq, mem_mask, rms_scale, q_w, kv_w, out_w):
        import jax, jax.numpy as jnp
        import numpy as np
        NUM_HEADS, NUM_KV, HEAD_DIM, WIDTH = (4, 1, 64, 256)
        MASK_FILL = -2.3819763e+38

        def _apply_rope(x, positions, max_wavelength=10000.0):
            d = x.shape[-1]
            freq_exp = 2.0 / d * jnp.arange(d // 2, dtype=jnp.float32)
            timescale = max_wavelength ** freq_exp
            radians = positions[..., None].astype(jnp.float32) / timescale
            radians = radians[..., None, :]
            sin, cos = (jnp.sin(radians), jnp.cos(radians))
            x1, x2 = jnp.split(x, 2, axis=-1)
            out = jnp.concatenate([x1 * cos - x2 * sin, x2 * cos + x1 * sin], axis=-1)
            return out.astype(x.dtype)

        def _rmsnorm(x, scale):
            var = jnp.mean(jnp.square(x.astype(jnp.float32)), axis=-1, keepdims=True)
            normed = x * jax.lax.rsqrt(var + 1e-06)
            return (normed * (1 + scale)).astype(x.dtype)
        B, S, _ = mem_seq.shape
        T = x.shape[1]
        G = NUM_HEADS // NUM_KV
        xn = _rmsnorm(x, rms_scale)
        mn = _rmsnorm(mem_seq, rms_scale)
        q = jnp.einsum('BTD,NDH->BTNH', xn, q_w)
        kv = jnp.einsum('BSD,cKDH->cBSKH', mn, kv_w)
        k, v = (kv[0], kv[1])
        q_pos = jnp.broadcast_to(jnp.arange(S, T + S), (B, T))
        k_pos = jnp.broadcast_to(jnp.arange(S), (B, S))
        q = _apply_rope(q, q_pos) * HEAD_DIM ** (-0.5)
        k = _apply_rope(k, k_pos)
        q = q.reshape(B, T, NUM_KV, G, HEAD_DIM)
        logits = jnp.einsum('BTKGH,BSKH->BKGTS', q, k, preferred_element_type=jnp.float32)
        masked = jnp.where(mem_mask[:, None, None, None, :], logits, MASK_FILL)
        probs = jax.nn.softmax(masked, axis=-1).astype(x.dtype)
        enc = jnp.einsum('BKGTS,BSKH->BTKGH', probs, v).reshape(B, T, NUM_HEADS, HEAD_DIM)
        return jnp.einsum('BTNH,NHD->BTD', enc, out_w)

    def _L0_attn_ref(x, Wq, Wk, Wv, Wo, qn_w, kn_w):
        import jax, jax.numpy as jnp
        import numpy as np
        NUM_HEADS = 16
        EPS = float(jnp.finfo(jnp.float32).eps)

        def rms_norm(x, w):
            ms = jnp.mean(x * x, axis=-1, keepdims=True)
            return x * jax.lax.rsqrt(ms + EPS) * w
        B, N, D = x.shape
        H = NUM_HEADS
        Dh = D // H
        scale = Dh ** (-0.5)

        def proj(W):
            return (x @ W.T).reshape(B, N, H, Dh).transpose(0, 2, 1, 3)
        q = rms_norm(proj(Wq), qn_w)
        k = rms_norm(proj(Wk), kn_w)
        v = proj(Wv)
        scores = jnp.einsum('bhnd,bhmd->bhnm', q, k) * scale
        attn = jax.nn.softmax(scores, axis=-1)
        out = jnp.einsum('bhnm,bhmd->bhnd', attn, v)
        out = out.transpose(0, 2, 1, 3).reshape(B, N, D)
        return out @ Wo.T

    def _L0_ffn_ref(x, Wg, W1, W2):
        import jax, jax.numpy as jnp
        import numpy as np
        B, S, D = x.shape
        E = Wg.shape[1]
        T = B * S
        cap = max(1, T // E)
        xt = x.reshape(T, D)
        logits = xt @ Wg
        probs = jax.nn.softmax(logits, axis=-1)
        pT = probs.T
        _, top_idx = jax.lax.top_k(pT, cap)
        sel = jnp.zeros((E, T), dtype=bool).at[jnp.arange(E)[:, None], top_idx].set(True)
        masked = jnp.where(sel, pT, -jnp.inf)
        assigned = sel.any(axis=0)
        tok2exp = jnp.where(assigned, jnp.argmax(masked, axis=0), jnp.argmax(pT, axis=0))
        weights = jnp.take_along_axis(probs, tok2exp[:, None], axis=1)[:, 0]
        out = jnp.zeros_like(xt)
        for e in range(E):
            gate = jnp.where(tok2exp == e, weights, 0.0)
            h = jax.nn.gelu(xt @ W1[e], approximate=False) @ W2[e]
            out = out + gate[:, None] * h
        return out.reshape(B, S, D)

    def _L1_xattn_ref(char_emb, subword_emb, Wq_c, bq_c, Wk_s, bk_s, Wv_s, bv_s, Wq_s, bq_s, Wk_c, bk_c, Wv_c, bv_c, Wg, bg):
        import jax, jax.numpy as jnp
        import numpy as np
        H = 256
        B = 8
        L_CHAR = 512
        L_SUB = 256

        def _linear(x, W, b):
            return jnp.einsum('blh,oh->blo', x, W) + b

        def _interp_linear(x, out_len):
            L_in = x.shape[1]
            pos = (jnp.arange(out_len, dtype=x.dtype) + 0.5) * (L_in / out_len) - 0.5
            pos = jnp.clip(pos, 0.0, L_in - 1)
            lo = jnp.floor(pos).astype(jnp.int32)
            hi = jnp.minimum(lo + 1, L_in - 1)
            w = (pos - lo.astype(x.dtype))[None, :, None]
            return x[:, lo] * (1 - w) + x[:, hi] * w
        h = char_emb.shape[-1]
        scale = 1.0 / jnp.sqrt(jnp.asarray(h, char_emb.dtype))
        Q_char = _linear(char_emb, Wq_c, bq_c)
        K_sub = _linear(subword_emb, Wk_s, bk_s)
        V_sub = _linear(subword_emb, Wv_s, bv_s)
        scores = jnp.einsum('bqh,bkh->bqk', Q_char, K_sub) * scale
        char2sub = jnp.einsum('bqk,bkh->bqh', jax.nn.softmax(scores, axis=-1), V_sub)
        Q_sub = _linear(subword_emb, Wq_s, bq_s)
        K_char = _linear(char_emb, Wk_c, bk_c)
        V_char = _linear(char_emb, Wv_c, bv_c)
        scores2 = jnp.einsum('bqh,bkh->bqk', Q_sub, K_char) * scale
        sub2char = jnp.einsum('bqk,bkh->bqh', jax.nn.softmax(scores2, axis=-1), V_char)
        L_char = char_emb.shape[1]
        if sub2char.shape[1] != L_char:
            sub2char = _interp_linear(sub2char, L_char)
        gate_in = jnp.concatenate([char2sub, sub2char], axis=-1)
        gate = jax.nn.sigmoid(jnp.einsum('blh,oh->blo', gate_in, Wg) + bg)
        return gate * char2sub + (1 - gate) * sub2char

    def _L1_attn_ref(x, Q_w, Q_b, K_w, K_b, V_w, V_b, O_w, O_b):
        import jax, jax.numpy as jnp
        import numpy as np
        import math
        N_HEADS, D_HEAD, D_MODEL = (16, 64, 256)
        B, S = (4, 512)
        NEG_MASK = -100000.0
        q = jnp.einsum('bpm,hmd->bphd', x, Q_w) + Q_b
        k = jnp.einsum('bpm,hmd->bphd', x, K_w) + K_b
        v = jnp.einsum('bpm,hmd->bphd', x, V_w) + V_b
        logits = jnp.einsum('bqhd,bkhd->bhqk', q, k) / math.sqrt(D_HEAD)
        s = logits.shape[-1]
        causal = jnp.triu(jnp.ones((s, s), dtype=bool), k=1)
        logits = jnp.where(causal, NEG_MASK, logits)
        scores = jax.nn.softmax(logits, axis=-1)
        attn = jnp.einsum('bhqk,bkhd->bqhd', scores, v)
        return jnp.einsum('bqhd,hdm->bqm', attn, O_w) + O_b

    def _L1_ffn_ref(x, Wr, br, W_up, b_up, W_down, b_down):
        import jax, jax.numpy as jnp
        import numpy as np
        B, S, H = (4, 512, 256)
        E = 8
        GS = 2
        NG = E // GS
        F = int(H * 4 * (2.0 / 3.0))
        b, s, h = x.shape
        n_tok = b * s
        k = n_tok // E
        xf = x.reshape(n_tok, h)
        logits = xf @ Wr + br
        Sm = jax.nn.softmax(logits, axis=-1)
        G_t, idx_t = jax.lax.top_k(Sm.T, k)
        G = G_t.T
        idx = idx_t.T
        tokens = xf[idx]
        group = jnp.arange(E) // GS
        Wu = W_up[group]
        bu = b_up[group]
        mid = jax.nn.silu(jnp.einsum('keh,ehf->kef', tokens, Wu) + bu)
        out = jnp.einsum('kef,efh->keh', mid, W_down) + b_down
        y = jnp.zeros_like(xf).at[idx].add(G[..., None] * out)
        return y.reshape(b, s, h)

    def _L2_xattn_ref(x, tab_x, tab_g, tab_b, vid_g, vid_b, Wq, Wk, Wv, q_g, q_b, k_g, k_b, Wo, bo):
        import jax, jax.numpy as jnp
        import numpy as np
        EPS = 1e-05

        def layernorm(x, g, b):
            mu = jnp.mean(x, axis=-1, keepdims=True)
            var = jnp.var(x, axis=-1, keepdims=True)
            return (x - mu) * jax.lax.rsqrt(var + EPS) * g + b
        DIM = 256
        CTX = 256
        HEADS = 12
        DHEAD = 64
        INNER = HEADS * DHEAD
        B = 4
        F = 512
        J = 256
        scale = DHEAD ** (-0.5)
        kv_in = layernorm(tab_x, tab_g, tab_b)
        q = layernorm(layernorm(x, vid_g, vid_b) @ Wq, q_g, q_b)
        k = layernorm(kv_in @ Wk, k_g, k_b)
        v = kv_in @ Wv
        split = lambda t: t.reshape(t.shape[0], t.shape[1], HEADS, DHEAD).transpose(0, 2, 1, 3)
        q, k, v = (split(q) * scale, split(k), split(v))
        sim = jnp.einsum('bhid,bhjd->bhij', q, k)
        attn = jax.nn.softmax(sim, axis=-1)
        out = jnp.einsum('bhij,bhjd->bhid', attn, v)
        out = out.transpose(0, 2, 1, 3).reshape(x.shape[0], x.shape[1], INNER)
        return out @ Wo + bo

    def _L2_attn_ref(x, norm_g, norm_b, Wq, Wkv, q_scale, k_scale, null_kv, Wout):
        import jax, jax.numpy as jnp
        import numpy as np
        import math
        B, N, DIM, H, DH, NNULL = (2, 512, 256, 16, 64, 2)
        SCALE = 8.0
        LN_EPS = 1e-05

        def _alibi_slopes(heads):
            start = 2.0 ** (-2.0 ** (-(math.log2(heads) - 3)))
            return np.array([start * start ** i for i in range(heads)], dtype=np.float32)

        def _l2norm(t):
            n = jnp.sqrt(jnp.sum(t * t, axis=-1, keepdims=True))
            return t / jnp.maximum(n, 1e-12)
        b, n, dim = x.shape
        h, dh, nn = (H, DH, NNULL)
        j = n + nn
        mu = jnp.mean(x, axis=-1, keepdims=True)
        var = jnp.mean((x - mu) ** 2, axis=-1, keepdims=True)
        xn = (x - mu) * jax.lax.rsqrt(var + LN_EPS) * norm_g + norm_b
        q = (xn @ Wq).reshape(b, n, h, dh).transpose(0, 2, 1, 3)
        kv = x @ Wkv
        k, v = jnp.split(kv, 2, axis=-1)
        k = k.reshape(b, n, h, dh).transpose(0, 2, 1, 3)
        v = v.reshape(b, n, h, dh).transpose(0, 2, 1, 3)
        null = null_kv.reshape(h, nn, 2, dh)
        nk = jnp.broadcast_to(null[:, :, 0, :][None], (b, h, nn, dh))
        nv = jnp.broadcast_to(null[:, :, 1, :][None], (b, h, nn, dh))
        k = jnp.concatenate([nk, k], axis=2)
        v = jnp.concatenate([nv, v], axis=2)
        q = _l2norm(q) * q_scale
        k = _l2norm(k) * k_scale
        sim = jnp.einsum('bhid,bhjd->bhij', q, k) * SCALE
        irow = jnp.arange(j - n, j)
        jcol = jnp.arange(j)
        bias = -jnp.abs(jcol[None, :] - irow[:, None]).astype(sim.dtype)
        slopes = jnp.asarray(_alibi_slopes(h))[:, None, None]
        sim = sim + slopes * bias
        causal = jnp.triu(jnp.ones((n, j), dtype=bool), k=j - n + 1)
        neg = jnp.finfo(sim.dtype).max
        sim = jnp.where(causal[None, None], -neg, sim)
        attn = jax.nn.softmax(sim, axis=-1)
        out = jnp.einsum('bhij,bhjd->bhid', attn, v)
        out = out.transpose(0, 2, 1, 3).reshape(b, n, h * dh)
        return out @ Wout

    def _L2_ffn_ref(x, w1_w, w1_s, w2_w, w2_s, h1_w, h1_s, h2_w, h2_s, w3_w, w3_s):
        import jax, jax.numpy as jnp
        import numpy as np
        D_IN, D_HID = (256, 1024)

        def _ternary(key, shape):
            return jax.random.randint(key, shape, -1, 2).astype(jnp.float32)

        def _tlin(x, w, s):
            return jnp.einsum('bsi,oi->bso', x, w) * s
        h = jax.nn.silu(_tlin(x, w1_w, w1_s)) * _tlin(x, w2_w, w2_s)
        h = jax.nn.gelu(_tlin(h, h1_w, h1_s), approximate=False)
        h = jax.nn.gelu(_tlin(h, h2_w, h2_s), approximate=False)
        return _tlin(h, w3_w, w3_s)

    def _L3_xattn_ref(q, k, v, Wq, bq, Wk, bk, Wv, bv, Wo, bo):
        import jax, jax.numpy as jnp
        import numpy as np
        D_MODEL = 256
        N_HEAD = 16
        D_K = D_MODEL // N_HEAD

        def _split_heads(x):
            B, S, _ = x.shape
            return x.reshape(B, S, N_HEAD, D_K).transpose(0, 2, 1, 3)
        qh = _split_heads(q @ Wq.T + bq)
        kh = _split_heads(k @ Wk.T + bk)
        vh = _split_heads(v @ Wv.T + bv)
        score = jnp.einsum('bhqd,bhkd->bhqk', qh, kh) / jnp.sqrt(jnp.float32(D_K))
        attn = jax.nn.softmax(score, axis=-1)
        out = jnp.einsum('bhqk,bhkd->bhqd', attn, vh)
        B, H, S, Dk = out.shape
        out = out.transpose(0, 2, 1, 3).reshape(B, S, H * Dk)
        return out @ Wo.T + bo

    def _L3_attn_ref(x, Wq, Wk, Wv, Wo, bo):
        import jax, jax.numpy as jnp
        import numpy as np
        DIM = 256
        HEADS = 16
        DIM_HEAD = 64
        INNER = HEADS * DIM_HEAD
        EPS = 1e-10

        def safe_softmax(s):
            m = jnp.max(s, axis=-1, keepdims=True)
            e = jnp.exp(s - m)
            return e / (jnp.sum(e, axis=-1, keepdims=True) + EPS)
        B, N, _ = x.shape
        scale = DIM_HEAD ** (-0.5)

        def split_heads(t):
            return t.reshape(B, N, HEADS, DIM_HEAD).transpose(0, 2, 1, 3)
        q = split_heads(x @ Wq.T)
        k = split_heads(x @ Wk.T)
        v = split_heads(x @ Wv.T)
        sim = jnp.einsum('bhid,bhjd->bhij', q, k) * scale
        attn = safe_softmax(sim)
        out = jnp.einsum('bhij,bhjd->bhid', attn, v)
        out = out.transpose(0, 2, 1, 3).reshape(B, N, INNER)
        return out @ Wo.T + bo

    def _L3_ffn_ref(x, packed_weight, weight_scale, bias):
        import jax, jax.numpy as jnp
        import numpy as np
        IN_F = 256
        OUT_F = 256
        B, S = (8, 1024)

        def _pack_ternary(tern):
            enc = (tern + 1.0).astype(jnp.int32).reshape(-1)
            return (enc[0::4] | enc[1::4] << 2 | enc[2::4] << 4 | enc[3::4] << 6).astype(jnp.int32)
        n = OUT_F * IN_F
        shifts = jnp.array([0, 2, 4, 6], dtype=jnp.int32)
        enc = (packed_weight[None, :] >> shifts[:, None] & 3).reshape(-1)[:n]
        w = (enc.astype(jnp.float32) - 1.0).reshape(OUT_F, IN_F) * weight_scale
        act_scale = 127.0 / jnp.maximum(jnp.max(jnp.abs(x), axis=-1, keepdims=True), 1e-05)
        x_dq = jnp.clip(jnp.round(x * act_scale), -128.0, 127.0) / act_scale
        return jnp.einsum('bsi,oi->bso', x_dq, w) + bias
    x = x + _L0_xattn_ref(_layernorm(x, axis=-1), ctx_1024, mask_BxS2_bk0, L0_xattn_rms_scale, L0_xattn_q_w, L0_xattn_kv_w, L0_xattn_out_w)
    x = x + _L0_attn_ref(_layernorm(x, axis=-1), L0_attn_Wq, L0_attn_Wk, L0_attn_Wv, L0_attn_Wo, L0_attn_qn_w, L0_attn_kn_w)
    x = x + _L0_ffn_ref(_layernorm(x, axis=-1), L0_ffn_Wg, L0_ffn_W1, L0_ffn_W2)
    x = x + _L1_xattn_ref(_layernorm(x, axis=-1), ctx_1024, L1_xattn_Wq_c, L1_xattn_bq_c, L1_xattn_Wk_s, L1_xattn_bk_s, L1_xattn_Wv_s, L1_xattn_bv_s, L1_xattn_Wq_s, L1_xattn_bq_s, L1_xattn_Wk_c, L1_xattn_bk_c, L1_xattn_Wv_c, L1_xattn_bv_c, L1_xattn_Wg, L1_xattn_bg)
    x = x + _L1_attn_ref(_layernorm(x, axis=-1), L1_attn_Q_w, L1_attn_Q_b, L1_attn_K_w, L1_attn_K_b, L1_attn_V_w, L1_attn_V_b, L1_attn_O_w, L1_attn_O_b)
    x = x + _L1_ffn_ref(_layernorm(x, axis=-1), L1_ffn_Wr, L1_ffn_br, L1_ffn_W_up, L1_ffn_b_up, L1_ffn_W_down, L1_ffn_b_down)
    x = x + _L2_xattn_ref(_layernorm(x, axis=-1), ctx_1024, L2_xattn_tab_g, L2_xattn_tab_b, L2_xattn_vid_g, L2_xattn_vid_b, L2_xattn_Wq, L2_xattn_Wk, L2_xattn_Wv, L2_xattn_q_g, L2_xattn_q_b, L2_xattn_k_g, L2_xattn_k_b, L2_xattn_Wo, L2_xattn_bo)
    x = x + _L2_attn_ref(_layernorm(x, axis=-1), L2_attn_norm_g, L2_attn_norm_b, L2_attn_Wq, L2_attn_Wkv, L2_attn_q_scale, L2_attn_k_scale, L2_attn_null_kv, L2_attn_Wout)
    x = x + _L2_ffn_ref(_layernorm(x, axis=-1), L2_ffn_w1_w, L2_ffn_w1_s, L2_ffn_w2_w, L2_ffn_w2_s, L2_ffn_h1_w, L2_ffn_h1_s, L2_ffn_h2_w, L2_ffn_h2_s, L2_ffn_w3_w, L2_ffn_w3_s)
    x = x + _L3_xattn_ref(_layernorm(x, axis=-1), ctx_1024, ctx_1024, L3_xattn_Wq, L3_xattn_bq, L3_xattn_Wk, L3_xattn_bk, L3_xattn_Wv, L3_xattn_bv, L3_xattn_Wo, L3_xattn_bo)
    x = x + _L3_attn_ref(_layernorm(x, axis=-1), L3_attn_Wq, L3_attn_Wk, L3_attn_Wv, L3_attn_Wo, L3_attn_bo)
    x = x + _L3_ffn_ref(_layernorm(x, axis=-1), L3_ffn_packed_weight, L3_ffn_weight_scale, L3_ffn_bias)
    return x

_drawn_inputs = setup_inputs


def setup_inputs(seed=0):
    import zlib

    import numpy as np

    out = dict(_drawn_inputs(seed))
    spreads = {'L0_attn_qn_w': (1.0, 0.2),
     'L0_attn_kn_w': (1.0, 0.2),
     'L1_attn_Q_b': (0.0, 0.1),
     'L1_attn_K_b': (0.0, 0.1),
     'L1_attn_V_b': (0.0, 0.1),
     'L1_attn_O_b': (0.0, 0.1),
     'L1_ffn_br': (0.0, 0.1),
     'L2_xattn_tab_g': (1.0, 0.2),
     'L2_xattn_tab_b': (0.0, 0.1),
     'L2_xattn_vid_g': (1.0, 0.2),
     'L2_xattn_vid_b': (0.0, 0.1),
     'L2_xattn_q_g': (1.0, 0.2),
     'L2_xattn_q_b': (0.0, 0.1),
     'L2_xattn_k_g': (1.0, 0.2),
     'L2_xattn_k_b': (0.0, 0.1),
     'L2_xattn_bo': (0.0, 0.1),
     'L2_attn_norm_g': (1.0, 0.2),
     'L2_attn_norm_b': (0.0, 0.1),
     'L2_attn_q_scale': (1.0, 0.2),
     'L2_attn_k_scale': (1.0, 0.2),
     'L3_xattn_bq': (0.0, 0.1),
     'L3_xattn_bk': (0.0, 0.1),
     'L3_xattn_bv': (0.0, 0.1),
     'L3_xattn_bo': (0.0, 0.1),
     'L3_ffn_bias': (0.0, 0.1)}
    factors = {}
    for name, (base, spread) in spreads.items():
        noise = np.random.default_rng([zlib.crc32(name.encode()), seed]).standard_normal(out[name].shape)
        drawn = base * np.exp(spread * noise) if base else spread * noise
        out[name] = jnp.asarray(drawn.astype(out[name].dtype))
    for name, factor in factors.items():
        out[name] = (out[name] * factor).astype(out[name].dtype)
    return out
```

```python
from contextlib import ExitStack

import numpy as np
import concourse.bass as bass
from concourse import mybir

ALU = mybir.AluOpType
ACT = mybir.ActivationFunctionType
AX = mybir.AxisListType
F32 = mybir.dt.float32
I32 = mybir.dt.int32
U8 = mybir.dt.uint8
BF16 = mybir.dt.bfloat16

DEBUG = False
STAGES = 12
FILL = 2.3819763e38
FMAX = float(np.finfo(np.float32).max)
COLS = [("L0_xattn_rms_scale", 2), ("L0_attn_qn_w", 1), ("L0_attn_kn_w", 1), ("L1_attn_Q_b", 8), ("L1_attn_K_b", 8),
        ("L1_attn_V_b", 8), ("L1_ffn_b_up", 24), ("L1_xattn_bq_c", 2), ("L1_xattn_bk_c", 2), ("L1_xattn_bk_s", 2),
        ("L1_xattn_bv_s", 2), ("L1_xattn_bq_s", 2), ("L1_xattn_bv_c", 2), ("L1_xattn_bg", 2), ("L2_xattn_tab_g", 2),
        ("L2_xattn_tab_b", 2), ("L2_xattn_vid_g", 2), ("L2_xattn_vid_b", 2), ("L2_xattn_q_g", 6), ("L2_xattn_q_b", 6),
        ("L2_xattn_k_g", 6), ("L2_attn_norm_g", 2), ("L2_attn_norm_b", 2), ("L2_attn_q_scale", 1),
        ("L2_attn_k_scale", 1), ("L2_ffn_w1_s", 8), ("L2_ffn_w2_s", 8), ("L2_ffn_h1_s", 8), ("L2_ffn_h2_s", 8),
        ("L3_xattn_bq", 2), ("L3_xattn_bk", 2), ("L3_xattn_bv", 2)]
CAT = {}
NCOL = 0
for _n, _c in COLS:
    CAT[_n] = (NCOL, _c)
    NCOL += _c


class Queue:

    def __init__(self, sem):
        self.sem, self.items, self.n, self.seen = sem, [], 0, {}

    def wait(self, *after):
        for t in after:
            if t is None:
                continue
            if isinstance(t, list):
                self.wait(*t)
                continue
            sem, value = t
            if self.seen.get(id(sem), 0) < value:
                self.seen[id(sem)] = value
                self.items.append(lambda e, sem=sem, value=value: e.wait_ge(sem, value))

    def do(self, fn, *after):
        self.wait(*after)
        self.n += 1
        self.items.append(lambda e: fn(e).then_inc(self.sem, 1))
        return (self.sem, self.n)

    def quiet(self, fn, *after):
        self.wait(*after)
        self.items.append(fn)

    def dma(self, sem, out, in_, *after):
        self.wait(*after)
        sem.n += 16
        self.items.append(lambda e: e.dma_start(out, in_).then_inc(sem.sem, 16))
        return (sem.sem, sem.n)

    def now(self):
        return (self.sem, self.n)

    def emit(self, e):
        for item in self.items:
            item(e)


class Landing:

    def __init__(self, sem):
        self.sem, self.n = sem, 0


class Slot:

    def __init__(self, ap, land=None):
        self.ap, self.land, self.free, self.full = ap, land, None, None


class Ring:
    def __init__(self, slots):
        self.slots, self.i = slots, 0

    def next(self):
        s = self.slots[self.i % len(self.slots)]
        self.i += 1
        return s


def was(tokens, key, i):
    return None if i < 0 else tokens[key, i]


def pipeline(n, stages):
    for t in range(n + len(stages) - 1):
        for k in reversed(range(len(stages))):
            if 0 <= t - k < n:
                stages[k](t - k)


def program(nc, A, out, dbg):
    with ExitStack() as ctx:
        build(nc, ctx, A, out, dbg)


def build(nc, ctx, A, out, dbg):
    cnt = [0]

    def sb(shape, dt=F32, scope=None):
        cnt[0] += 1
        return (scope or ctx).enter_context(nc.sbuf_tensor(f"t{cnt[0]}", shape, dt))

    def sem(name):
        return ctx.enter_context(nc.semaphore(name))

    PE, DV, AC, PO, SP = [Queue(sem(n)) for n in ("s_pe", "s_dv", "s_ac", "s_po", "s_sp")]
    compute = [PE, DV, AC, PO]
    big = ctx.enter_context(nc.psum_tensor("psum", [128, 4096], F32))
    bank = [big[:, 512 * i:512 * (i + 1)] for i in range(8)]

    def mm(out, lhsT, rhs, start, stop, *after, sig=False, skip=False):
        f = lambda e: e.matmul(out, lhsT, rhs, start=start, stop=stop, skip_group_check=skip)
        if sig:
            return PE.do(f, *after)
        PE.quiet(f, *after)

    def tr(out, in_, ident, *after, sig=False):
        f = lambda e: e.transpose(out, in_, ident)
        if sig:
            return PE.do(f, *after)
        PE.quiet(f, *after)

    def act(out, in_, fn, *after, bias=0.0, scale=1.0, acc=None):
        if acc is None:
            return AC.do(lambda e: e.activation(out, in_, fn, bias=bias, scale=scale), *after)
        return AC.do(lambda e: e.activation(out, in_, fn, bias=bias, scale=scale, accum_out=acc), *after)

    def tt(q, out, a, b, op, *after):
        return q.do(lambda e: e.tensor_tensor(out, a, b, op), *after)

    def ts(q, out, a, s1, s2, op0, op1, *after):
        if op1 is None:
            return q.do(lambda e: e.tensor_scalar(out, a, s1, None, op0), *after)
        return q.do(lambda e: e.tensor_scalar(out, a, s1, s2, op0, op1), *after)

    def stt(out, a, s, b, op0, op1, *after):
        return DV.do(lambda e: e.scalar_tensor_tensor(out=out, in0=a, scalar=s, in1=b, op0=op0, op1=op1), *after)

    def ttr(out, a, b, op0, op1, init, acc, *after):
        return DV.do(lambda e: e.tensor_tensor_reduce(out=out, in0=a, in1=b, scale=1.0, scalar=init,
                                                      op0=op0, op1=op1, accum_out=acc), *after)

    def red(out, in_, op, *after, negate=False):
        return DV.do(lambda e: e.tensor_reduce(out, in_, AX.X, op, negate=negate), *after)

    def cp(q, out, in_, *after):
        if q is AC:
            return AC.do(lambda e: e.activation(out, in_, ACT.Copy), *after)
        return q.do(lambda e: e.tensor_copy(out, in_), *after)

    def recip(out, in_, *after):
        return DV.do(lambda e: e.reciprocal(out, in_), *after)

    def memset(q, out, v, *after):
        return q.do(lambda e: e.memset(out, v), *after)

    def barrier():
        ends = [q.now() for q in compute]
        for q in compute + [SP]:
            q.wait(ends)
        return ends

    x = sb([128, 16, 256])
    xn = sb([128, 16, 256])
    xT = sb([128, 2, 2048])
    ident = sb([128, 128])
    ones = sb([128, 128])
    negh = sb([128, 64])
    mv = sb([128, 16, 2])
    rs = sb([128, 16])
    st = sb([128, 16, 6])
    cols = sb([128, NCOL])
    mvc = sb([128, 64, 2, 2])
    l_x, l_c, l_out = Landing(sem("l_x")), Landing(sem("l_c")), Landing(sem("l_out"))
    l_w = [Landing(sem("l_w0")), Landing(sem("l_w1"))]
    xtok = [None] * 16
    for g in range(4):
        t = SP.dma(l_x, x[:, 4 * g:4 * g + 4, :],
                   A["x"].rearrange("b s d -> (b s) d").rearrange("(i p) d -> p i d", p=128)[:, 4 * g:4 * g + 4, :])
    xtok = [t] * 16
    t_cols = SP.dma(l_c, cols[:], A["cols"])

    def col(name, c=None):
        o, n = CAT[name]
        return cols[:, o:o + n] if c is None else cols[:, o + c:o + c + 1]

    t = memset(PO, ident[:], 0.0)
    t_ident = PO.do(lambda e: e.affine_select(out=ident[:], in_=ident[:], compare_op=ALU.not_equal, fill=1.0,
                                              base=0, pattern=[[-1, 128]], channel_multiplier=1), t)
    t_ones = memset(PO, ones[:], 1.0)
    t_negh = memset(PO, negh[:], -0.5)
    lower = sb([128, 128])
    t_lower = memset(PO, lower[:], 1.0)
    t_lower = PO.do(lambda e: e.affine_select(out=lower[:], in_=lower[:], compare_op=ALU.is_gt, fill=0.0,
                                              base=0, pattern=[[1, 128]], channel_multiplier=-1), t_lower)
    t_cst = t_negh
    rms1 = sb([128, 2])
    t_rms1 = ts(DV, rms1[:], col("L0_xattn_rms_scale"), 1.0, None, ALU.add, None, t_cols)

    def loader(scope, par):
        def take(dram, dt=F32, split=2):
            K, M = dram.shape
            c = max(1, K // 128)
            ap = sb([min(K, 128), c, M], dt, scope)
            src = dram.rearrange("(c p) m -> p c m", c=c)
            for cc in range(0, c, split):
                t = SP.dma(l_w[par], ap[:, cc:cc + split, :], src[:, cc:cc + split, :])
            return ap, t
        return take

    def normed(srct, g, src, dst, eps, rms=False):
        sl = slice(4 * g, 4 * g + 4)
        for i in range(4 * g, 4 * g + 4):
            t = DV.do(lambda e, i=i: e.bn_stats(st[:, i, :], src[:, i, :]), srct[i])
            t = DV.do(lambda e, i=i: e.bn_aggr(mv[:, i, :], st[:, i, :]), t)
        if rms:
            t = tt(PO, rs[:, sl], mv[:, sl, 0], mv[:, sl, 0], ALU.mult, t)
            t = tt(PO, rs[:, sl], rs[:, sl], mv[:, sl, 1], ALU.add, t)
            t = ts(PO, rs[:, sl], rs[:, sl], eps, None, ALU.add, None, t)
        else:
            t = ts(PO, rs[:, sl], mv[:, sl, 1], eps, None, ALU.add, None, t)
        t = tt(PO, rs[:, sl], rs[:, sl], negh[:, 0:4], ALU.pow, t, t_negh)
        return t

    def apply_norm(t, g, src, dst, rms=False):
        toks = []
        for i in range(4 * g, 4 * g + 4):
            if rms:
                toks.append(ts(DV, dst[:, i, :], src[:, i, :], rs[:, i:i + 1], None, ALU.mult, None, t))
            else:
                toks.append(ts(DV, dst[:, i, :], src[:, i, :], mv[:, i, 0:1], rs[:, i:i + 1],
                               ALU.subtract, ALU.mult, t))
        return toks

    def turned(toks, g, src, dst, slots, sc=None, bi=None, waits=None):
        outs = []
        for c in range(2):
            s = slots.next()
            for k in range(4):
                i = 4 * g + k
                t = tr(s.ap[:, k * 128:(k + 1) * 128], src[:, i, c * 128:(c + 1) * 128], ident[:],
                       toks[k], s.free, t_ident, sig=(k == 3))
            d = dst[:, c, g * 512:(g + 1) * 512]
            if sc is None:
                s.free = cp(AC if c else DV, d, s.ap[:], t)
            else:
                s.free = ts(DV, d, s.ap[:], sc[:, c:c + 1], bi[:, c:c + 1] if bi is not None else 0.0,
                            ALU.mult, ALU.add, t, waits)
            outs.append(s.free)
        return outs

    def layernorm(second=None, keep=None):
        slots = Ring([Slot(b) for b in bank[0:8]])
        st1, st2, st3, out, out2 = {}, {}, {}, {}, {}

        def a(g):
            st1[g] = normed(xtok, g, x, xn, 1e-5)

        def b(g):
            st2[g] = apply_norm(st1[g], g, x, xn)
            for k in range(4):
                xntok[4 * g + k] = st2[g][k]

        def c(g):
            if second is None:
                out[g] = turned(st2[g], g, xn, xT, slots)
            elif keep is not None:
                out2[g] = turned(st2[g], g, xn, keep, slots)

        def d(g):
            if second:
                st3[g] = normed(xntok, g, xn, xn, second[0], second[1])

        def e(g):
            if second:
                tk = apply_norm(st3[g], g, xn, xn, second[1]) if keep is None else \
                    apply_norm([st3[g], out2[g]], g, xn, xn, second[1])
                st2[g] = tk

        def f(g):
            if second:
                out[g] = turned(st2[g], g, xn, xT, slots, second[2], second[3], [t_rms1, t_cols])

        xntok = [None] * 16
        pipeline(4, [a, b, c, d, e, f])
        PE.wait(DV.now(), AC.now())
        return out, out2

    def add_x(i, ps, *after):
        xtok[i] = tt(DV, x[:, i, :], x[:, i, :], ps, ALU.add, xtok[i], *after)
        return xtok[i]

    def ctx_ring(scope, n, tok=True, turn=True, name=""):
        slots = []
        for k in range(n):
            c = sb([128, 2, 256], F32, scope) if tok else None
            r = sb([1, 256], F32, scope) if tok else None
            T = sb([128, 2, 257], F32, scope) if turn else None
            slots.append(Slot((c, r, T), Landing(sem(f"l_{name}{k}"))))
        return Ring(slots)

    def load_ctx(ring, b):
        s = ring.next()
        c, r, T = s.ap
        if c is not None:
            s.full = SP.dma(s.land, c[:], A["ctx"][b, 0:256, :].rearrange("(k p) d -> p k d", p=128), s.free)
            s.full = SP.dma(s.land, r[:], A["ctx"][b, 256:257, :], s.free)
        if T is not None:
            s.full = SP.dma(s.land, T[:], A["ctxT"][b].rearrange("(c p) s -> p c s", p=128), s.free)
        return s

    def l0_xattn(par):
        with ExitStack() as sc:
            take = loader(sc, par)
            wq, _ = take(A["L0x_q"])
            wkv, _ = take(A["L0x_kv"])
            wo, tw = take(A["L0x_o"])
            l_m = Landing(sem("l_m"))
            m32 = sb([128, 64 * 257 // 4], I32, sc)
            m8 = m32[:].bitcast(U8)
            t_m8 = SP.dma(l_m, m32[:], A["mask"].rearrange("(a n) -> a n", a=1).to_broadcast([128, 64 * 257 // 4]))
            rope_q = sb([128, 2, 256], F32, sc)
            rope_k = sb([128, 2, 2, 64], F32, sc)
            rope_t = sb([64, 2, 64], F32, sc)
            SP.dma(l_m, rope_q[:], A["rope_q"])
            SP.dma(l_m, rope_k[:], A["rope_k"])
            SP.dma(l_m, rope_t[:], A["rope_t"])
            tailT = sb([128, 2, 64], F32, sc)
            tail = sb([64, 256], F32, sc)
            SP.dma(l_m, tailT[:], A["tailT"].rearrange("(c p) s -> p c s", p=128))
            t_m = SP.dma(l_m, tail[:], A["ctx"][:, 256, :])
            out, _ = layernorm(second=(1e-6, True, rms1, None))
            t_w1 = []
            for c in range(2):
                t_w1.append(ts(DV, wkv[:, c, :], wkv[:, c, :], rms1[:, c:c + 1], None, ALU.mult, None, tw, t_rms1))
            qT = sb([64, 16, 4, 4, 32], F32, sc)
            otok = [sb([128, 256], F32, sc) for _ in range(2)]
            bR = Ring([Slot(b) for b in bank[0:4]])
            tA = [sb([128, 4, 64], F32, sc) for _ in range(2)]
            tB = [sb([128, 4, 64], F32, sc) for _ in range(2)]
            state = {}

            def q1(i):
                s = bR.next()
                for c in range(2):
                    t = mm(s.ap[:, 0:256], xT[:, c, i * 128:(i + 1) * 128], wq[:, c, :], c == 0, c == 1,
                           s.free, out[i // 4], tw, sig=(c == 1))
                state[i] = (s, t)

            def q2(i):
                s, t = state[i]
                a, b = tA[i % 2], tB[i % 2]
                v = s.ap[:, 0:256].rearrange("p (h d) -> p h d", h=4)
                cq = rope_q[:, 0, :].rearrange("p (h d) -> p h d", h=4)
                sq = rope_q[:, 1, :].rearrange("p (h d) -> p h d", h=4)
                w = [was(state, "q3", i - 2)]
                t1 = tt(DV, a[:], v, cq, ALU.mult, t, t_m, w)
                t2 = tt(DV, b[:, :, 0:32], v[:, :, 32:64], sq[:, :, 0:32], ALU.mult)
                t3 = tt(DV, b[:, :, 32:64], v[:, :, 0:32], sq[:, :, 32:64], ALU.mult)
                s.free = t3
                state["q2", i] = tt(DV, a[:], a[:], b[:], ALU.add, t1, t2, t3)

            def q3(i):
                a = tA[i % 2]
                s = bR.next()
                for h in range(4):
                    t = tr(s.ap[0:64, h * 128:(h + 1) * 128], a[:, h, :], ident[:], s.free, state["q2", i],
                           sig=(h == 3))
                state["q3", i] = t
                s.free = cp(AC, qT[:, i].rearrange("p j h q -> p h j q"),
                            s.ap[0:64, :].rearrange("p (h j q) -> p h j q", h=4, j=4), t)
                state["qT", i] = s.free

            pipeline(16, [q1, q2, q3])
            kTt = sb([64, 64], F32, sc)
            vt = sb([64, 64], F32, sc)
            vt1 = sb([1, 64, 64], F32, sc)
            tmp = sb([64, 3, 64], F32, sc)
            stt_ = sb([64, 6], F32, sc)
            mvt = sb([64, 4], F32, sc)
            t = DV.do(lambda e: e.bn_stats(stt_[:], tail[:]), t_m)
            t = DV.do(lambda e: e.bn_aggr(mvt[:, 0:2], stt_[:]), t)
            t = tt(PO, mvt[:, 2:3], mvt[:, 0:1], mvt[:, 0:1], ALU.mult, t)
            t = tt(PO, mvt[:, 2:3], mvt[:, 2:3], mvt[:, 1:2], ALU.add, t)
            t = ts(PO, mvt[:, 2:3], mvt[:, 2:3], 1e-6, None, ALU.add, None, t)
            tr_ = tt(PO, mvt[:, 3:4], mvt[:, 2:3], negh[0:64, 0:1], ALU.pow, t)
            s = bR.next()
            for c in range(2):
                t = mm(s.ap[0:64, 0:128], tailT[:, c, :], wkv[:, c, :], c == 0, c == 1, s.free, t_w1, t_m, sig=(c == 1))
            t1 = act(vt[:], s.ap[0:64, 64:128], ACT.Copy, t, tr_, scale=mvt[:, 3:4])
            t2 = act(tmp[:, 0, :], s.ap[0:64, 0:64], ACT.Copy, scale=mvt[:, 3:4])
            s.free = t2
            t3 = tt(DV, tmp[:, 1, :], tmp[:, 0, :], rope_t[:, 0, :], ALU.mult, t2)
            t4 = tt(DV, tmp[:, 2, 0:32], tmp[:, 0, 32:64], rope_t[:, 1, 0:32], ALU.mult)
            t5 = tt(DV, tmp[:, 2, 32:64], tmp[:, 0, 0:32], rope_t[:, 1, 32:64], ALU.mult)
            t6 = tt(DV, tmp[:, 1, :], tmp[:, 1, :], tmp[:, 2, :], ALU.add, t3, t4, t5)
            s = bR.next()
            t7 = tr(s.ap[0:64, 0:64], tmp[:, 1, :], ident[0:64, 0:64], s.free, t6, sig=True)
            s.free = t_kTt = cp(DV, kTt[:], s.ap[0:64, 0:64], t7)
            t_vt1 = SP.dma(l_m, vt1[:], vt[:], t1)

            ring = ctx_ring(sc, 4, name="a")
            kv = [sb([128, 2, 128], F32, sc) for _ in range(4)]
            kr = [sb([128, 2, 64], F32, sc) for _ in range(2)]
            kr2 = [sb([128, 2, 64], F32, sc) for _ in range(2)]
            kT = [sb([64, 257], F32, sc) for _ in range(2)]
            mb = [sb([128, 257], F32, sc) for _ in range(2)]
            S = [sb([128, 257], F32, sc) for _ in range(2)]
            PT = [sb([128, 384], F32, sc) for _ in range(2)]
            sm = sb([128, 64, 4], F32, sc)
            stc = sb([128, 2, 2, 6], F32, sc)
            rr = sb([128, 64, 2], F32, sc)
            oT = [sb([128, 2, 128], F32, sc) for _ in range(2)]
            psA = Slot(bank[0])
            psK = Slot(bank[1])
            psS = Ring([Slot(bank[2]), Slot(bank[3])])
            psT = Ring([Slot(bank[4]), Slot(bank[5])])
            psO = Slot(bank[6])
            psX = Slot(bank[7])
            for q in (PE,):
                q.wait(AC.now(), DV.now())
            B = {}

            def st0(b):
                B[b] = load_ctx(ring, b)

            def st1_(b):
                s = B[b]
                c, r, T = s.ap
                k = b % 2
                for kt in range(2):
                    t = DV.do(lambda e, kt=kt: e.bn_stats(stc[:, k, kt, :], c[:, kt, :]), s.full, was(B, "rr", b - 2))
                    t = DV.do(lambda e, kt=kt: e.bn_aggr(mvc[:, b, kt, :], stc[:, k, kt, :]), t)
                t = tt(PO, rr[:, b, :], mvc[:, b, :, 0], mvc[:, b, :, 0], ALU.mult, t)
                t = tt(PO, rr[:, b, :], rr[:, b, :], mvc[:, b, :, 1], ALU.add, t)
                t = ts(PO, rr[:, b, :], rr[:, b, :], 1e-6, None, ALU.add, None, t)
                B["rr", b] = tt(PO, rr[:, b, :], rr[:, b, :], negh[:, 0:2], ALU.pow, t)
                for kt in range(2):
                    for cc in range(2):
                        t = mm(psA.ap[:, kt * 128:(kt + 1) * 128], T[:, cc, kt * 128:(kt + 1) * 128], wkv[:, cc, :],
                               cc == 0, cc == 1, psA.free, s.full, t_w1, sig=(cc == 1 and kt == 1))
                B["kvps", b] = t

            def st2_(b):
                k = b % 2
                for kt in range(2):
                    t = act(kv[b % 4][:, kt, :], psA.ap[:, kt * 128:(kt + 1) * 128], ACT.Copy, B["kvps", b], B["rr", b],
                            was(B, "pv", b - 4), scale=rr[:, b, kt:kt + 1])
                psA.free = t
                B[b].free = [B["kvps", b], B["rr", b]]
                B["kv", b] = t
                kk = kv[b % 4][:, :, 0:64]
                t1 = tt(PO, kr[k][:], kk, rope_k[:, 0, :, :], ALU.mult, t, t_m, was(B, "psK", b - 2))
                t2 = tt(PO, kr2[k][:, :, 0:32], kk[:, :, 32:64], rope_k[:, 1, :, 0:32], ALU.mult)
                t3 = tt(PO, kr2[k][:, :, 32:64], kk[:, :, 0:32], rope_k[:, 1, :, 32:64], ALU.mult)
                t = tt(PO, kr[k][:], kr[k][:], kr2[k][:], ALU.add, t1, t2, t3)
                for kt in range(2):
                    t = tr(psK.ap[0:64, kt * 128:(kt + 1) * 128], kr[k][:, kt, :], ident[:], psK.free, t, sig=(kt == 1)) \
                        if kt else (tr(psK.ap[0:64, 0:128], kr[k][:, 0, :], ident[:], psK.free, t) or t)
                B["psK", b] = t

            def st3_(b):
                k = b % 2
                B["mb", b] = ts(PO, mb[k][:], m8[:, b * 257:(b + 1) * 257], 1.0, FILL, ALU.subtract, ALU.mult,
                                t_m8, was(B, "S", b - 2))
                t = cp(AC, kT[k][:, 0:256], psK.ap[0:64, 0:256], B["psK", b], was(B, "psS", b - 2))
                psK.free = t
                t2 = cp(AC, kT[k][:, 256:257], kTt[:, b:b + 1], t_kTt)
                s = psS.next()
                i, j = b // 4, b % 4
                t = mm(s.ap[:, 0:257], qT[:, i, j].rearrange("p h q -> p (h q)"), kT[k][:], True, True, t, t2, s.free,
                       state["qT", i], sig=True)
                B["psS", b] = t
                B["psSs", b] = s

            def st4_(b):
                k = b % 2
                s = B["psSs", b]
                t = ttr(S[k][:], s.ap[:, 0:257], mb[k][:], ALU.add, ALU.max, -3.4e38, sm[:, b, 0:1], B["psS", b],
                        B["mb", b], was(B, "psT", b - 2))
                B["S", b] = s.free = t
                t = ts(DV, sm[:, b, 1:2], sm[:, b, 0:1], -1.0, None, ALU.mult, None, t)
                t = act(S[k][:], S[k][:], ACT.Exp, t, bias=sm[:, b, 1:2], acc=sm[:, b, 2:3])
                B["sum", b] = t
                B["ri", b] = recip(sm[:, b, 3:4], sm[:, b, 2:3], t)

            def st5_(b):
                k = b % 2
                s = psT.next()
                tr(s.ap[:, 0:128], S[k][:, 0:128], ident[:], B["sum", b], s.free)
                tr(s.ap[:, 128:256], S[k][:, 128:256], ident[:])
                t = tr(s.ap[0:1, 256:384], S[k][:, 256:257], ident[:], sig=True)
                B["psT", b] = t
                t1 = cp(AC, PT[k][:, 0:256], s.ap[:, 0:256], t, was(B, "pv", b - 2))
                s.free = cp(AC, PT[k][0:1, 256:384], s.ap[0:1, 256:384])
                B["PT", b] = s.free

            def st6_(b):
                k = b % 2
                mm(psO.ap[:, 0:64], PT[k][:, 0:128], kv[b % 4][:, 0, 64:128], True, False, B["PT", b], psO.free)
                mm(psO.ap[:, 0:64], PT[k][:, 128:256], kv[b % 4][:, 1, 64:128], False, False)
                t = mm(psO.ap[:, 0:64], PT[k][0:1, 256:384], vt1[:, b, :], False, True, t_vt1, sig=True)
                B["pv", b] = t
                i, j = b // 4, b % 4
                for h in range(4):
                    psO.free = ts(DV, otok[i % 2][32 * j:32 * j + 32, 64 * h:64 * h + 64], psO.ap[32 * h:32 * h + 32, 0:64],
                                  sm[32 * h:32 * h + 32, b, 3:4], None, ALU.mult, None, t, B["ri", b], was(B, "oX", i - 2))
                B["o", b] = psO.free

            def st7_(b):
                if b % 4 < 3:
                    return
                i = b // 4
                for c in range(2):
                    t = tr(psX.ap[:, c * 128:(c + 1) * 128], otok[i % 2][:, c * 128:(c + 1) * 128], ident[:],
                           B["o", b], psX.free, sig=(c == 1))
                B["oX", i] = t
                B["oT", i] = cp(AC, oT[i % 2][:], psX.ap[:, 0:256].rearrange("p (c t) -> p c t", c=2), t,
                                was(B, "out", i - 2))

            def st8_(b):
                if b % 4 < 3:
                    return
                i = b // 4
                for c in range(2):
                    t = mm(psX.ap[:, 256:512], oT[i % 2][:, c, :], wo[:, c, :], c == 0, c == 1, B["oT", i],
                           sig=(c == 1))
                B["out", i] = t
                psX.free = add_x(i, psX.ap[:, 256:512], t)

            pipeline(64, [st0, st1_, st2_, st3_, st4_, st5_, st6_, st7_, st8_])

    def self_attention(sc, prods, hd, ready, wo, tw, scale=1.0, keep=None, bias=None, null=None, brow=None,
                       ring=None, eps=0.0):
        nch = 16 * hd // 128
        off = 2 if null else 0
        nk = 32 + off
        S = [sb([128, 16, nk], F32, sc) for _ in range(2)]
        bd = [sb([128, 16, 128], F32, sc) for _ in range(2)]
        nm = sb([128, 2, 3, 16], F32, sc)
        oT = [sb([128, nch, 128], F32, sc) for _ in range(2)]
        Pn = [sb([128, 32], F32, sc) for _ in range(2)] if null else None
        PnT = [sb([32, 128], F32, sc) for _ in range(2)] if null else None
        tz = [memset(PO, bd[k][:], 0.0) for k in range(2)]
        ps4 = big[:, 0:2048].rearrange("p (s k) -> p s k", s=16)
        psS = Slot(ps4)
        psO = Slot(big[:, 2048:2048 + nch * 128].rearrange("p (c t) -> p c t", c=nch))
        B = {}

        def scores(i):
            qT, kT, v, toks = ready[i]
            for s in range(16):
                par, ch = s // nch, s % nch
                r = par * hd
                t = mm(ps4[:, s, :], qT[r:r + hd, ch, :], kT[r:r + hd, ch, :], True, True, toks, psS.free, sig=(s == 15))
            B["S", i] = t
            if null:
                z = ring.next()
                for ch in range(nch):
                    t = mm(z.ap[:, 4 * ch:4 * ch + 4], qT[:, ch, :], null[0][:, ch, :], True, True, z.free, null[2],
                           sig=(ch == nch - 1))
                B["S", i] = t
                B["N", i] = []
                for par in range(2):
                    z.free = act(S[i % 2][:, par * nch:(par + 1) * nch, 0:2],
                                 z.ap[:, 0:32].rearrange("p (c a n) -> p a c n", a=2, n=2)[:, par], ACT.Copy,
                                 t, was(B, "bd", i - 2), scale=null[3])
                    B["N", i].append(z.free)

        def soft(i):
            k = i % 2
            s_, free = S[k], was(B, "bd", i - 2)
            ext = []
            for j in range(4):
                o = s_[32 * j:32 * j + 32, :, off:nk]
                p = ps4[32 * j:32 * j + 32, :, 32 * j:32 * j + 32]
                if keep is None:
                    ext.append(act(o, p, ACT.Copy, B["S", i], free, scale=scale))
                else:
                    m = keep[32 * j:32 * j + 32, :].unsqueeze(1).to_broadcast([32, 16, 32])
                    ext.append(stt(o, p, scale, m, ALU.mult, ALU.mult, B["S", i], free))
            psS.free = ext
            if null:
                ext = ext + B["N", i]
            if bias is not None:
                b_ = bias[:] if null else bias[:].unsqueeze(1).to_broadcast([128, 16, 32])
                ext = [tt(PO, s_[:], s_[:], b_, ALU.add, ext, t_cst)]
            m0, m1, m2 = nm[:, k, 0, :], nm[:, k, 1, :], nm[:, k, 2, :]
            t = red(m0, s_[:], ALU.max, ext)
            t = tt(PO, s_[:], s_[:], m0.unsqueeze(2).to_broadcast([128, 16, nk]), ALU.subtract, t)
            t = act(s_[:], s_[:], ACT.Exp, t)
            t2 = red(m1, s_[:], ALU.add, t)
            if eps:
                t2 = ts(DV, m1, m1, eps, None, ALU.add, None, t2)
            t2 = recip(m2, m1, t2)
            t = tt(PO, s_[:], s_[:], m2.unsqueeze(2).to_broadcast([128, 16, nk]), ALU.mult, t2)
            B["P", i] = t

        def turn(i):
            k = i % 2
            if null:
                t = cp(AC, Pn[k][:].rearrange("p (s n) -> p s n", n=2), S[k][:, :, 0:2], B["P", i], was(B, "PnT", i - 2))
                z = ring.next()
                t = tr(z.ap[0:32, 0:128], Pn[k][:], ident[:], t, z.free, sig=True)
                B["PnT", i] = t
                z.free = B["Pn", i] = cp(AC, PnT[k][:], z.ap[0:32, 0:128], t, was(B, "O", i - 2))
            tk = []
            for j in range(4):
                tk.append(DV.do(lambda e, j=j: e.transpose(bd[k][32 * j:32 * j + 32, :, 32 * j:32 * j + 32],
                                                           S[k][32 * j:32 * j + 32, :, off:nk]),
                                B["P", i], tz[k], was(B, "O", i - 2)))
            B["bd", i] = tk + ([B["Pn", i]] if null else [])

        def values(i):
            k = i % 2
            qT, kT, v, toks = ready[i]
            for ch in range(nch):
                if null:
                    mm(psO.ap[:, ch, :], null[1][:, ch, :], PnT[k][:], ch % 4 == 0, False, B["bd", i], psO.free, null[2],
                       skip=True)
                for par in range(128 // hd):
                    h = ch * (128 // hd) + par
                    last = ch == nch - 1 and par == 128 // hd - 1
                    t = mm(psO.ap[par * hd:(par + 1) * hd, ch, :], v[:, h * hd:(h + 1) * hd], bd[k][:, par * nch + ch, :],
                           not null, True, B["bd", i], psO.free, sig=last, skip=bool(null))
            B["O", i] = t
            psO.free = []
            half = max(nch // 2, 4)
            for n, c0 in enumerate(range(0, nch, half)):
                psO.free.append(cp([AC, DV][n], oT[k][:, c0:c0 + half, :], psO.ap[:, c0:c0 + half, :], t,
                                   was(B, "X", i - 2)))

        def project(i):
            k = i % 2
            z = ring.next()
            if brow is not None:
                mm(z.ap[:, 0:256], ones[0:1, :], brow[0], True, False, brow[1], z.free, t_ones)
            for ch in range(nch):
                t = mm(z.ap[:, 0:256], oT[k][:, ch, :], wo[:, ch, :], ch == 0 and brow is None, ch == nch - 1,
                       psO.free if ch == 0 else None, z.free, tw, sig=(ch == nch - 1))
            B["X", i] = t
            z.free = add_x(i, z.ap[:, 0:256], t)

        pipeline(16, prods + [scores, soft, turn, values, project])

    def cbc(name, c0, c1, n):
        o, _ = CAT[name]
        return cols[:, o + c0:o + c1].unsqueeze(2).to_broadcast([128, c1 - c0, n])

    def l0_attn(par):
        with ExitStack() as sc:
            take = loader(sc, par)
            wqk, _ = take(A["L0a_qk"])
            wv, _ = take(A["L0a_v"])
            wo, tw = take(A["L0a_o"])
            out, _ = layernorm()
            ring = Ring([Slot(bank[6]), Slot(bank[7]), Slot(bank[5])])
            sq = [sb([128, 512], F32, sc) for _ in range(2)]
            ms = sb([128, 2, 32], F32, sc)
            qk = [sb([128, 32, 32], F32, sc) for _ in range(2)]
            v = [sb([128, 16, 32], F32, sc) for _ in range(6)]
            qT = [sb([128, 4, 128], F32, sc) for _ in range(3)]
            kT = [sb([128, 4, 128], F32, sc) for _ in range(3)]
            tz = [memset(PO, a[:], 0.0) for a in qk + v]
            B, ready = {}, {}

            def p1(i):
                s1, s2 = ring.next(), ring.next()
                for c in range(2):
                    t = mm(s1.ap[:], xT[:, c, i * 128:(i + 1) * 128], wqk[:, c, :], c == 0, c == 1, s1.free,
                           out[i // 4], tw, sig=(c == 1))
                for c in range(2):
                    t2 = mm(s2.ap[:, 0:256], xT[:, c, i * 128:(i + 1) * 128], wv[:, c, :], c == 0, c == 1, s2.free,
                            sig=(c == 1))
                k = i % 2
                B["v", i] = s2.free = cp(AC, v[i % 6][:, :, 0:16], s2.ap[:, 0:256].rearrange("p (h d) -> p h d", h=16), t2, tz)
                t3 = act(sq[k][:], s1.ap[:], ACT.Square, t, was(B, "ms", i - 2))
                t3 = red(ms[:, k, :], sq[k][:].rearrange("p (h d) -> p h d", h=32), ALU.add, t3, was(B, "qk", i - 2))
                B["ms", i] = t3
                t3 = ts(PO, ms[:, k, :], ms[:, k, :], 1.0 / 16, float(np.finfo(np.float32).eps), ALU.mult, ALU.add, t3)
                t3 = tt(PO, ms[:, k, :], ms[:, k, :], negh[:, 0:32], ALU.pow, t3)
                s1.free = B["qk", i] = tt(DV, qk[k][:, :, 0:16], s1.ap[:].rearrange("p (h d) -> p h d", h=32),
                                          ms[:, k, :].unsqueeze(2).to_broadcast([128, 32, 16]), ALU.mult, t3, tz,
                                          was(B, "tr", i - 2))

            def p2(i):
                k = i % 2
                flat = qk[k][:].rearrange("p (c h) d -> p c (h d)", c=8)
                tk = []
                for w, (dst, nw) in enumerate(((qT, "L0_attn_qn_w"), (kT, "L0_attn_kn_w"))):
                    z = ring.next()
                    for c in range(4):
                        t = tr(z.ap[:, c * 128:(c + 1) * 128], flat[:, 4 * w + c, :], ident[:], B["qk", i], z.free,
                               sig=(c == 3))
                    z.free = act(dst[i % 3][:].rearrange("p c t -> p (c t)"), z.ap[:], ACT.Copy, t, t_cols,
                                 scale=col(nw, 0))
                    tk.append(z.free)
                B["tr", i] = t
                ready[i] = (qT[i % 3], kT[i % 3], v[i % 6][:].rearrange("p h d -> p (h d)"), tk + [B["v", i]])

            self_attention(sc, [p1, p2], 32, ready, wo, tw, scale=0.25, ring=ring)

    def rows(scope, par, name, n=256):
        r = sb([1, n], F32, scope)
        t = SP.dma(l_w[par], r[:], A[name].rearrange("(a n) -> a n", a=1))
        return r, t

    def fold_row(scope, slot, bcols, wo, nch, row, tw):
        r = sb([1, 256], F32, scope)
        for ch in range(nch):
            t = mm(slot.ap[0:1, 0:256], bcols(ch), wo[:, ch, :], ch == 0, ch == nch - 1, tw, t_cols, slot.free,
                   sig=(ch == nch - 1))
        slot.free = t = tt(DV, r[:], slot.ap[0:1, 0:256], row, ALU.add, t, tw)
        return r[:], t

    def wide_attn(par, pre, bias, eps, scale, keep, brow_name):
        with ExitStack() as sc:
            take = loader(sc, par)
            wq, _ = take(A[pre + "_q"], split=1)
            wk, _ = take(A[pre + "_k"], split=1)
            wv, _ = take(A[pre + "_v"], split=1)
            wo, _ = take(A[pre + "_o"], split=4)
            bo, tw = rows(sc, par, brow_name)
            kp = ng = None
            if keep:
                kp, ng = sb([128, 32], F32, sc), sb([128, 32], F32, sc)
                SP.dma(l_w[par], kp[:], A["keep"])
                tw = SP.dma(l_w[par], ng[:], A["neg"])
            DV.wait(tw)
            PO.wait(tw)
            out, _ = layernorm()
            ring = Ring([Slot(bank[6]), Slot(bank[7])])
            if bias:
                brow = fold_row(sc, ring.next(), lambda ch: col("L1_attn_V_b", ch), wo, 8, bo[:], tw)
            else:
                brow = (bo[:], tw)
            q = [sb([128, 8, 256], F32, sc) for _ in range(2)]
            k = [sb([128, 8, 256], F32, sc) for _ in range(2)]
            v = [sb([128, 2, 1024], F32, sc) for _ in range(4)]
            B, ready = {}, {}

            def p1(i):
                if i % 2:
                    return
                u = i // 2
                tk = []
                for w, (dst, wt, bn) in enumerate(((q, wq, "L1_attn_Q_b"), (k, wk, "L1_attn_K_b"))):
                    for m in range(0, 8, 2):
                        z = ring.next()
                        for mo in range(2):
                            for c in range(2):
                                t = mm(z.ap[:, mo * 256:(mo + 1) * 256], wt[:, c, (m + mo) * 128:(m + mo + 1) * 128],
                                       xT[:, c, u * 256:(u + 1) * 256], c == 0, c == 1, z.free, out[u // 2], tw,
                                       sig=(c == 1 and mo == 1))
                        z.free = []
                        for mo in range(2):
                            d, p = dst[u % 2][:, m + mo, :], z.ap[:, mo * 256:(mo + 1) * 256]
                            if bias and m % 4 == 0:
                                z.free.append(act(d, p, ACT.Identity, t, t_cols, bias=col(bn, m + mo)))
                            elif bias:
                                z.free.append(ts(DV, d, p, col(bn, m + mo), None, ALU.add, None, t, t_cols))
                            else:
                                z.free.append(cp(AC if m % 4 else DV, d, p, t))
                        tk += z.free
                for n in range(2):
                    for hf in range(2):
                        z = ring.next()
                        for c in range(2):
                            t = mm(z.ap[:], xT[:, c, u * 256 + n * 128:u * 256 + (n + 1) * 128],
                                   wv[:, c, hf * 512:(hf + 1) * 512], c == 0, c == 1, z.free, sig=(c == 1))
                        z.free = cp(AC if hf else DV, v[u % 4][:, n, hf * 512:(hf + 1) * 512], z.ap[:], t)
                        tk.append(z.free)
                for n in range(2):
                    ready[i + n] = (q[u % 2][:, :, n * 128:(n + 1) * 128], k[u % 2][:, :, n * 128:(n + 1) * 128],
                                    v[u % 4][:, n, :], tk)

            self_attention(sc, [p1], 64, ready, wo, tw, scale=scale, keep=kp, bias=ng, brow=brow, ring=ring, eps=eps)

    def l1_attn(par):
        wide_attn(par, "L1a", True, 0.0, 1.0, True, "L1_attn_O_b")

    def l3_attn(par):
        wide_attn(par, "L3a", False, 1e-10, 0.125, False, "L3_attn_bo")

    def top256(sc, probs, t_p):
        T = lambda shape, dt=F32: sb(shape, dt, sc)
        thr, cand, pred, cmp_, cnt = T([128, 8], I32), T([128, 8], I32), T([128, 8], I32), T([128, 8, 16]), T([128, 8])
        gt, eq, sel = T([128, 8, 16]), T([128, 8, 16]), T([128, 8, 16])
        ca, cb = T([128, 8, 16]), T([128, 8, 16])
        slot = Slot(bank[0])
        t = memset(DV, thr[:], 0)
        for bit in range(29, -1, -1):
            t = DV.do(lambda e, bit=bit: e.tensor_scalar(cand[:], thr[:], 1 << bit, None, ALU.bitwise_or), t)
            t = tt(DV, cmp_[:], probs, cand[:].bitcast(F32).unsqueeze(2).to_broadcast([128, 8, 16]), ALU.is_ge, t, t_p)
            t = red(cnt[:], cmp_[:], ALU.add, t)
            t = mm(slot.ap[:, 0:8], ones[:], cnt[:], True, True, t, t_ones, sig=True)
            t = ts(DV, pred[:], slot.ap[:, 0:8], 256.0, None, ALU.is_ge, None, t)
            t = DV.do(lambda e: e.copy_predicated(thr[:], pred[:], cand[:]), t)
        tb = thr[:].bitcast(F32).unsqueeze(2).to_broadcast([128, 8, 16])
        t1 = tt(DV, gt[:], probs, tb, ALU.is_gt, t)
        t2 = tt(DV, eq[:], probs, tb, ALU.is_equal)
        t = red(cnt[:], gt[:], ALU.add, t1)
        t3 = memset(DV, ca[:], 0.0)
        t3 = cp(DV, ca[:, :, 1:16], eq[:, :, 0:15], t2, t3)
        a, b = ca, cb
        for d in (1, 2, 4, 8):
            t4 = cp(DV, b[:, :, 0:d], a[:, :, 0:d], t3)
            t3 = tt(DV, b[:, :, d:16], a[:, :, d:16], a[:, :, 0:16 - d], ALU.add, t3)
            t3 = [t3, t4]
            a, b = b, a
        s2 = Slot(bank[1])
        mm(s2.ap[:, 0:128], lower[:], eq[:].rearrange("p e i -> p (e i)"), True, False, t2, t_lower)
        t5 = mm(s2.ap[:, 0:128], ones[:], a[:].rearrange("p e i -> p (e i)"), False, True, t3, sig=True)
        t6 = mm(slot.ap[:, 0:8], ones[:], cnt[:], True, True, t, sig=True)
        t6 = ts(DV, cnt[:], slot.ap[:, 0:8], -1.0, 256.0, ALU.mult, ALU.add, t6)
        t = tt(DV, sel[:], s2.ap[:, 0:128].rearrange("p (e i) -> p e i", e=8),
               cnt[:].unsqueeze(2).to_broadcast([128, 8, 16]), ALU.is_lt, t5, t6)
        t = tt(DV, sel[:], sel[:], eq[:], ALU.mult, t)
        t = tt(DV, sel[:], sel[:], gt[:], ALU.add, t)
        return sel, t

    def router(sc, out, wg, tw, brow):
        probs = sb([128, 8, 16], F32, sc)
        m = sb([128, 2, 16], F32, sc)
        z = Slot(bank[2])
        for i in range(16):
            if brow is not None:
                mm(z.ap[:, 8 * i:8 * i + 8], ones[0:1, :], brow, True, False, tw)
            for c in range(2):
                t = mm(z.ap[:, 8 * i:8 * i + 8], xT[:, c, i * 128:(i + 1) * 128], wg[:, c, :],
                       c == 0 and brow is None, c == 1, out[i // 4], tw, sig=(c == 1 and i == 15))
        pv = z.ap[:, 0:128].rearrange("p (i e) -> p i e", e=8)
        pr = probs[:].rearrange("p e i -> p i e")
        t2 = red(m[:, 0, :], pv, ALU.max, t)
        t = tt(DV, pr, pv, m[:, 0, :].unsqueeze(2).to_broadcast([128, 16, 8]), ALU.subtract, t, t2)
        t = act(probs[:], probs[:], ACT.Exp, t)
        t2 = red(m[:, 0, :], pr, ALU.add, t)
        t2 = recip(m[:, 1, :], m[:, 0, :], t2)
        t = tt(DV, probs[:], probs[:], m[:, 1, :].unsqueeze(1).to_broadcast([128, 8, 16]), ALU.mult, t2)
        return probs, t

    def l0_ffn(par):
        with ExitStack() as sc:
            take = loader(sc, par)
            wg, tw = take(A["L0f_g"])
            out, _ = layernorm()
            PE.wait(DV.now(), AC.now())
            probs, tp = router(sc, out, wg, tw, None)
            sel, t = top256(sc, probs[:], tp)
            T = lambda shape: sb(shape, F32, sc)
            un, key, mx, oh, run, gate = T([128, 16]), T([128, 8, 16]), T([128, 16]), T([128, 8, 16]), T([128, 16]), T([128, 8, 16])
            sT = sel[:].rearrange("p e i -> p i e")
            bc = lambda a: a.unsqueeze(1).to_broadcast([128, 8, 16])
            t2 = red(un[:], sT, ALU.max, t)
            t2 = ts(DV, un[:], un[:], -1.0, 1.0, ALU.mult, ALU.add, t2)
            t2 = tt(DV, sel[:], sel[:], bc(un[:]), ALU.max, t2)
            t3 = tt(DV, key[:], sel[:], probs[:], ALU.mult, t2)
            t4 = ts(DV, gate[:], sel[:], -1.0, None, ALU.add, None, t2)
            t3 = tt(DV, key[:], key[:], gate[:], ALU.add, t3, t4)
            t4 = red(mx[:], key[:].rearrange("p e i -> p i e"), ALU.max, t3)
            t4 = tt(DV, oh[:], key[:], bc(mx[:]), ALU.is_equal, t4)
            t5 = memset(DV, run[:], 1.0)
            for e in range(8):
                t6 = tt(DV, gate[:, e, :], oh[:, e, :], run[:], ALU.mult, t4, t5)
                t5 = tt(DV, run[:], run[:], gate[:, e, :], ALU.subtract, t6)
            t_gate = tt(DV, gate[:], gate[:], probs[:], ALU.mult, t5)

            w1 = Ring([Slot(T([128, 2, 512]), Landing(sem(f"l_f{k}"))) for k in range(3)])
            w2 = Ring([Slot(T([128, 4, 256]), Landing(sem(f"l_g{k}"))) for k in range(3)])
            hT = Ring([Slot(T([128, 4, 512])) for _ in range(3)])
            hb = Ring([Slot(bank[k]) for k in range(4)])
            ob = Ring([Slot(bank[k]) for k in range(4, 8)])
            PE.wait(DV.now())
            E, B = {}, {}

            def load(e):
                if e < 8:
                    a, b = w1.next(), w2.next()
                    a.full = SP.dma(a.land, a.ap[:], A["L0f_1"][e].rearrange("(c p) m -> p c m", p=128), a.free)
                    b.full = SP.dma(b.land, b.ap[:], A["L0f_2"][e].rearrange("(c p) m -> p c m", p=128), b.free)
                    E[e] = (a, b)
            for e in range(2):
                load(e)

            def up(n):
                e, g = n // 4, n % 4
                if g == 0:
                    load(e + 2)
                a, _ = E[e]
                h = hT.next()
                tk = []
                for m in range(4):
                    z = hb.next()
                    for c in range(2):
                        t = mm(z.ap[:], a.ap[:, c, m * 128:(m + 1) * 128], xT[:, c, g * 512:(g + 1) * 512], c == 0, c == 1,
                               a.full, z.free, sig=(c == 1))
                    z.free = act(h.ap[:, m, :], z.ap[:], ACT.Gelu, t, h.free)
                    tk.append(z.free)
                a.free = t
                B[n] = (h, tk)

            def down(n):
                e, g = n // 4, n % 4
                _, b = E[e]
                h, tk = B[n]
                for u in range(2):
                    z = ob.next()
                    for v in range(2):
                        for k in range(4):
                            t = mm(z.ap[:, v * 256:(v + 1) * 256], h.ap[:, k, (2 * u + v) * 128:(2 * u + v + 1) * 128],
                                   b.ap[:, k, :], k == 0, k == 3, tk, b.full, z.free, sig=(k == 3 and v == 1))
                    for v in range(2):
                        i = 4 * g + 2 * u + v
                        xtok[i] = z.free = stt(x[:, i, :], z.ap[:, v * 256:(v + 1) * 256], gate[:, e, i:i + 1],
                                               x[:, i, :], ALU.mult, ALU.add, t, t_gate, xtok[i])
                b.free = t
                h.free = t

            pipeline(32, [up, down])

    def l1_ffn(par):
        F = 682
        with ExitStack() as sc:
            take = loader(sc, par)
            wg, _ = take(A["L1f_r"])
            br, _ = rows(sc, par, "L1_ffn_br", 8)
            bd, tw = None, None
            T = lambda shape: sb(shape, F32, sc)
            bd = T([1, 2048])
            tw = SP.dma(l_w[par], bd[:], A["L1_ffn_b_down"].rearrange("(a e) n -> a (e n)", a=1))
            out, _ = layernorm()
            PE.wait(DV.now(), AC.now())
            probs, tp = router(sc, out, wg, tw, br[:])
            gate, t = top256(sc, probs[:], tp)
            t_gate = tt(DV, gate[:], gate[:], probs[:], ALU.mult, t)
            w1 = Ring([Slot(T([128, 2, F]), Landing(sem(f"l_h{k}"))) for k in range(2)])
            w2 = Ring([Slot((T([128, 5, 256]), T([42, 256])), Landing(sem(f"l_i{k}"))) for k in range(4)])
            hT = Ring([Slot(T([128, 6, 512])) for _ in range(3)])
            hb = Ring([Slot(bank[k]) for k in range(4)])
            ob = Ring([Slot(bank[k]) for k in range(4, 8)])
            PE.wait(DV.now())
            E, B = {}, {}

            def load(n):
                if n < 4:
                    a = w1.next()
                    a.full = SP.dma(a.land, a.ap[:], A["L1f_up"][n].rearrange("(c p) m -> p c m", p=128), a.free)
                    E["up", n] = a
                    for e in (2 * n, 2 * n + 1):
                        b = w2.next()
                        SP.dma(b.land, b.ap[0][:], A["L1f_down"][e, 0:640, :].rearrange("(c p) m -> p c m", p=128), b.free)
                        b.full = SP.dma(b.land, b.ap[1][:], A["L1f_down"][e, 640:682, :])
                        E["down", e] = b
            load(0)

            def up(n):
                q, g = n // 4, n % 4
                if g == 0:
                    load(q + 1)
                a = E["up", q]
                h = hT.next()
                tk = []
                for m in range(6):
                    z = hb.next()
                    M = 128 if m < 5 else 42
                    for c in range(2):
                        t = mm(z.ap[0:M, :], a.ap[:, c, m * 128:m * 128 + M], xT[:, c, g * 512:(g + 1) * 512],
                               c == 0, c == 1, a.full, z.free, sig=(c == 1))
                    z.free = act(h.ap[0:M, m, :], z.ap[0:M, :], ACT.Silu, t, h.free, t_cols,
                                 bias=col("L1_ffn_b_up", 6 * q + m)[0:M])
                    tk.append(z.free)
                a.free = t
                B[n] = (h, tk)

            def down(n):
                q, g = n // 4, n % 4
                h, tk = B[n]
                for e in (2 * q, 2 * q + 1):
                    b = E["down", e]
                    for u in range(2):
                        z = ob.next()
                        for v in range(2):
                            o = z.ap[:, v * 256:(v + 1) * 256]
                            mm(o, ones[0:1, :], bd[0:1, e * 256:(e + 1) * 256], True, False, z.free)
                            for k in range(6):
                                M = 128 if k < 5 else 42
                                t = mm(o, h.ap[0:M, k, (2 * u + v) * 128:(2 * u + v + 1) * 128],
                                       b.ap[0][:, k, :] if k < 5 else b.ap[1][:], False, k == 5, tk, b.full,
                                       sig=(k == 5 and v == 1))
                        for v in range(2):
                            i = 4 * g + 2 * u + v
                            xtok[i] = z.free = stt(x[:, i, :], z.ap[:, v * 256:(v + 1) * 256], gate[:, e, i:i + 1],
                                                   x[:, i, :], ALU.mult, ALU.add, t, t_gate, xtok[i])
                    b.free = t
                h.free = t

            pipeline(16, [up, down])

    def project_T(slots, w, src, dst, bias, g, w_t, s_t, nk=2, M=2, dst_t=None, scale=None):
        tk = []
        for m in range(M):
            z = slots.next()
            for c in range(nk):
                t = mm(z.ap[:], w[:, c, m * 128:(m + 1) * 128], src[:, c, g * 512:(g + 1) * 512], c == 0, c == nk - 1,
                       z.free, w_t, s_t, sig=(c == nk - 1))
            d = dst[:, m, g * 512:(g + 1) * 512]
            if bias is None:
                z.free = cp(AC if m else DV, d, z.ap[:], t, dst_t)
            elif m % 2:
                z.free = act(d, z.ap[:], ACT.Identity, t, t_cols, dst_t, bias=col(bias, m))
            else:
                z.free = ts(DV, d, z.ap[:], col(bias, m), None, ALU.add, None, t, t_cols, dst_t)
            tk.append(z.free)
        return tk

    def l1_xattn(par):
        with ExitStack() as sc:
            take = loader(sc, par)
            w = {}
            for n in ("qc", "ks", "vs", "qs", "kc", "vc", "g"):
                w[n], tw = take(A["L1x_" + n])
            wlo = sb([128, 2], F32, sc)
            tw = SP.dma(l_w[par], wlo[:], A["lerp"])
            DV.wait(tw)
            ring_c = Ring([Slot((sb([128, 4, 2, 256], F32, sc), sb([1, 4, 256], F32, sc)), Landing(sem(f"l_j{k}")))
                           for k in range(3)])
            ring_t = Ring([Slot((sb([128, 4, 2, 257], F32, sc), sb([128, 2, 4, 64], F32, sc)), Landing(sem(f"l_m{k}")))
                           for k in range(2)])
            B = {}

            def load_t(i):
                if i >= 16:
                    return
                s = ring_t.next()
                T, sel = s.ap
                for cc in range(2):
                    SP.dma(s.land, sel[:, cc], A["selT"][cc * 128:(cc + 1) * 128, 4 * i:4 * i + 4, :], s.free)
                for j in range(4):
                    s.full = SP.dma(s.land, T[:, j], A["ctxT"][4 * i + j].rearrange("(c p) s -> p c s", p=128))
                B["t", i] = s

            def load_c(i):
                s = ring_c.next()
                c, r = s.ap
                SP.dma(s.land, r[:], A["ctx"][4 * i:4 * i + 4, 256, :].rearrange("(a j) d -> a j d", a=1), s.free)
                for j in range(4):
                    s.full = SP.dma(s.land, c[:, j], A["ctx"][4 * i + j, 0:256, :].rearrange("(k p) d -> p k d", p=128))
                B["c", i] = s
            load_t(0)
            out, _ = layernorm()
            slots = Ring([Slot(b) for b in bank])
            X1, X2, Q1, K1 = [sb([128, 2, 2048], F32, sc) for _ in range(4)]
            bq = sb([1, 2048], F32, sc)
            qbk = sb([128, 16], F32, sc)
            Vc = xn
            tX1, tX2, tQ1, tK1, tV, tbq, tr_ = {}, {}, {}, {}, {}, {}, {}
            for g in range(4):
                tX1[g] = project_T(slots, w["qc"], xT, X1, "L1_xattn_bq_c", g, tw, out[g])
                tX2[g] = project_T(slots, w["kc"], xT, X2, "L1_xattn_bk_c", g, tw, out[g])
            for g in range(4):
                tQ1[g] = project_T(slots, w["ks"], X1, Q1, None, g, tw, tX1[g])
                tK1[g] = project_T(slots, w["qs"], X2, K1, None, g, tw, tX2[g])
                z = slots.next()
                for c in range(2):
                    t = mm(z.ap[0:1, :], col("L1_xattn_bq_s", c), X2[:, c, g * 512:(g + 1) * 512], c == 0, c == 1, z.free,
                           t_cols, tX2[g], sig=(c == 1))
                tbq[g] = z.free = cp(AC, bq[:, g * 512:(g + 1) * 512], z.ap[0:1, :], t)
                z = slots.next()
                for k in range(4):
                    i = 4 * g + k
                    for c in range(2):
                        t = mm(z.ap[:, k:k + 1], X1[:, c, i * 128:(i + 1) * 128], col("L1_xattn_bk_s", c), c == 0, c == 1,
                               z.free, tX1[g], sig=(c == 1 and k == 3))
                tr_[g] = z.free = cp(DV, qbk[:, 4 * g:4 * g + 4], z.ap[:, 0:4], t)
                for u in range(2):
                    z = slots.next()
                    for k in range(2):
                        i = 4 * g + 2 * u + k
                        for c in range(2):
                            t = mm(z.ap[:, k * 256:(k + 1) * 256], xT[:, c, i * 128:(i + 1) * 128], w["vc"][:, c, :],
                                   c == 0, c == 1, z.free, sig=(c == 1 and k == 1))
                    z.free = cp(AC, Vc[:, 4 * g + 2 * u:4 * g + 2 * u + 2, :],
                                z.ap[:].rearrange("p (k d) -> p k d", k=2), t)
                    tV[4 * g + 2 * u] = tV[4 * g + 2 * u + 1] = z.free
            t_all = [AC.now(), DV.now(), PE.now()]
            PcT, s2cT = X1, X2
            S = [sb([128, 257], F32, sc) for _ in range(2)]
            PT = [sb([128, 384], F32, sc) for _ in range(2)]
            S2 = [sb([128, 2, 32], F32, sc) for _ in range(2)]
            P2 = [sb([128, 32], F32, sc) for _ in range(2)]
            bd = [sb([128, 128], F32, sc) for _ in range(2)]
            sm = sb([128, 16, 12], F32, sc)
            tz = [memset(PO, bd[k][:], 0.0) for k in range(2)]

            def a1(i):
                load_c(i)
                load_t(i + 1)
                s = B["t", i]
                T, sel = s.ap
                z = slots.next()
                for j in range(4):
                    for cc in range(2):
                        t = mm(z.ap[32 * j:32 * j + 32, 0:257], Q1[:, cc, i * 128 + 32 * j:i * 128 + 32 * j + 32],
                               T[:, j, cc, :], cc == 0, cc == 1, z.free, s.full, tQ1[i // 4], sig=(cc == 1 and j == 3))
                B["z1", i] = (z, t)
                z = slots.next()
                for j in range(4):
                    for lh in range(2):
                        o = z.ap[32 * j:32 * j + 32, 32 * lh:32 * lh + 32]
                        tok = slice(i * 128 + 32 * j, i * 128 + 32 * j + 32)
                        for cc in range(2):
                            mm(o, sel[:, cc, j, 32 * lh:32 * lh + 32], K1[:, cc, tok], cc == 0, False, z.free,
                               tK1[i // 4])
                        t = mm(o, ones[0:1, 0:32], bq[:, tok], False, True, tbq[i // 4], sig=(lh == 1 and j == 3))
                s.free = t
                B["z2", i] = (z, t)

            def a2(i):
                k = i % 2
                z, t = B["z1", i]
                m = lambda n: sm[:, i, n:n + 1]
                z.free = t = ts(DV, S[k][:], z.ap[:, 0:257], qbk[:, i:i + 1], None, ALU.add, None, t, tr_[i // 4],
                                was(B, "T", i - 2))
                t = red(m(0), S[k][:], ALU.max, t)
                t = ts(DV, m(0), m(0), -0.0625, None, ALU.mult, None, t)
                t = act(S[k][:], S[k][:], ACT.Exp, t, bias=m(0), scale=0.0625, acc=m(1))
                z, t2 = B["z2", i]
                sm2 = sm[:, i, 4:6]
                t2 = red(sm2, z.ap[:, 0:64].rearrange("p (l k) -> p l k", l=2), ALU.max, t2)
                z.free = t2 = tt(DV, S2[k][:], z.ap[:, 0:64].rearrange("p (l k) -> p l k", l=2),
                                 sm2.unsqueeze(2).to_broadcast([128, 2, 32]), ALU.subtract, t2, was(B, "P2", i - 2))
                t2 = act(S2[k][:], S2[k][:], ACT.Exp, t2, scale=0.0625)
                t = recip(m(2), m(1), t)
                B["P", i] = ts(DV, S[k][:], S[k][:], m(2), None, ALU.mult, None, t)
                t2 = red(sm[:, i, 6:8], S2[k][:], ALU.add, t2)
                t2 = recip(sm[:, i, 8:10], sm[:, i, 6:8], t2)
                t2 = tt(DV, sm[:, i, 10:12], sm[:, i, 8:10], wlo[:], ALU.mult, t2, tw)
                t2 = ts(DV, S2[k][:, 0, :], S2[k][:, 0, :], sm[:, i, 10:11], None, ALU.mult, None, t2)
                t2 = stt(P2[k][:], S2[k][:, 1, :], sm[:, i, 11:12], S2[k][:, 0, :], ALU.mult, ALU.add, t2,
                         was(B, "bd", i - 2))
                B["P2", i] = t2
                tk = []
                for j in range(4):
                    tk.append(DV.do(lambda e, j=j: e.transpose(bd[k][32 * j:32 * j + 32, 32 * j:32 * j + 32],
                                                               P2[k][32 * j:32 * j + 32, :]),
                                    t2, tz[k], was(B, "s2", i - 2)))
                B["bd", i] = tk

            def a3(i):
                k = i % 2
                z = slots.next()
                tr(z.ap[:, 0:128], S[k][:, 0:128], ident[:], B["P", i], z.free)
                tr(z.ap[:, 128:256], S[k][:, 128:256], ident[:])
                B["T", i] = t = tr(z.ap[0:1, 256:384], S[k][:, 256:257], ident[:], sig=True)
                t1 = cp(AC, PT[k][:, 0:256], z.ap[:, 0:256], t, was(B, "pc", i - 2))
                z.free = B["PT", i] = cp(AC, PT[k][0:1, 256:384], z.ap[0:1, 256:384])
                z = slots.next()
                for m in range(2):
                    t = mm(z.ap[:, m * 128:(m + 1) * 128], Vc[:, i, m * 128:(m + 1) * 128], bd[k][:], True, True,
                           z.free, tV[i], B["bd", i], sig=(m == 1))
                B["s2", i] = t
                for m in range(2):
                    z.free = act(s2cT[:, m, i * 128:(i + 1) * 128], z.ap[:, m * 128:(m + 1) * 128], ACT.Identity, t,
                                 t_all, bias=col("L1_xattn_bv_c", m))
                B["s2c", i] = z.free

            def a4(i):
                k = i % 2
                s = B["c", i]
                c, r = s.ap
                z = slots.next()
                for m in range(2):
                    for j in range(4):
                        o = z.ap[:, m * 128 + 32 * j:m * 128 + 32 * j + 32]
                        for kt in range(2):
                            mm(o, c[:, j, kt, m * 128:(m + 1) * 128], PT[k][:, kt * 128 + 32 * j:kt * 128 + 32 * j + 32],
                               kt == 0, False, B["PT", i], s.full, z.free)
                        t = mm(o, r[0:1, j, m * 128:(m + 1) * 128], PT[k][0:1, 256 + 32 * j:256 + 32 * j + 32],
                               False, True, sig=(j == 3 and m == 1))
                s.free = B["pc", i] = t
                z.free = B["PcT", i] = cp(AC, PcT[:, :, i * 128:(i + 1) * 128],
                                          z.ap[:, 0:256].rearrange("p (m t) -> p m t", m=2), t, t_all)

            pipeline(16, [a1, a2, a3, a4])
            c2sT, gT = Q1, K1
            t_a = PE.now()
            fin = {}
            tc = {}
            for g in range(4):
                tc[g] = project_T(slots, w["vs"], PcT, c2sT, "L1_xattn_bv_s", g, tw, [B["PcT", 4 * g + k] for k in range(4)],
                                  dst_t=t_a)

            def g1(g):
                sl = slice(g * 512, (g + 1) * 512)
                tk = []
                for m in range(2):
                    z = slots.next()
                    for c in range(4):
                        src = (c2sT if c < 2 else s2cT)[:, c % 2, sl]
                        t = mm(z.ap[:], w["g"][:, c, m * 128:(m + 1) * 128], src, c == 0, c == 3, z.free, tc[g],
                               B["s2c", 4 * g + 3], sig=(c == 3))
                    z.free = act(gT[:, m, sl], z.ap[:], ACT.Sigmoid, t, t_cols, bias=col("L1_xattn_bg", m))
                    tk.append(z.free)
                for m in range(2):
                    d = c2sT[:, m, sl]
                    t = tt(DV, d, d, s2cT[:, m, sl], ALU.subtract, tk)
                    t = tt(PO, d, d, gT[:, m, sl], ALU.mult, t)
                    t = tt(DV, d, d, s2cT[:, m, sl], ALU.add, t)
                    fin[g, m] = t

            def g2(g):
                for k in range(0, 4, 2):
                    z = slots.next()
                    for v in range(2):
                        for m in range(2):
                            i = 4 * g + k + v
                            t = tr(z.ap[:, v * 256 + m * 128:v * 256 + (m + 1) * 128], c2sT[:, m, i * 128:(i + 1) * 128],
                                   ident[:], fin[g, 0], fin[g, 1], z.free, sig=(m == 1 and v == 1))
                    for v in range(2):
                        z.free = add_x(4 * g + k + v, z.ap[:, v * 256:(v + 1) * 256], t)

            pipeline(4, [g1, g2])

    def l2_xattn(par):
        with ExitStack() as sc:
            take = loader(sc, par)
            wq, _ = take(A["L2x_q"])
            wk, _ = take(A["L2x_k"])
            wv, _ = take(A["L2x_v"])
            wo, _ = take(A["L2x_o"])
            kb, _ = take(A["L2x_kb"], split=6)
            bo, _ = rows(sc, par, "L2_xattn_bo")
            tailc = sb([64, 256], F32, sc)
            tw = SP.dma(l_w[par], tailc[:], A["ctx"][:, 256, :])
            for q in (DV, AC):
                q.wait(tw)
            ring = Ring([Slot((sb([128, 2, 256], F32, sc), sb([1, 256], F32, sc)), Landing(sem(f"l_k{k}")))
                         for k in range(4)])
            out, _ = layernorm(second=(1e-5, False, col("L2_xattn_vid_g"), col("L2_xattn_vid_b")))
            slots = Ring([Slot(b) for b in bank])
            t3 = sb([128, 2, 2], F32, sc)
            wkT = sb([128, 6, 256], F32, sc)
            G = sb([128, 2, 256], F32, sc)
            t = red(t3[:, 0, :], wk[:], ALU.add, tw)
            t = ts(DV, t3[:, 1, :], t3[:, 0, :], 1.0 / 768, None, ALU.mult, None, t)
            for c in range(2):
                t_wk = ts(DV, wk[:, c, :], wk[:, c, :], t3[:, 1, c:c + 1], None, ALU.subtract, None, t)
            for n in range(3):
                z = slots.next()
                for v in range(2):
                    for c in range(2):
                        t = tr(z.ap[:, v * 256 + c * 128:v * 256 + (c + 1) * 128],
                               wk[:, c, (2 * n + v) * 128:(2 * n + v + 1) * 128], ident[:], t_wk, z.free,
                               sig=(v == 1 and c == 1))
                z.free = t_wkT = cp(AC, wkT[:, 2 * n:2 * n + 2, :], z.ap[:].rearrange("p (v c) -> p v c", v=2), t)
            for c in range(2):
                z = slots.next()
                for n in range(6):
                    t = mm(z.ap[:, 0:256], wkT[:, n, c * 128:(c + 1) * 128], wkT[:, n, :], n == 0, n == 5, t_wkT, z.free,
                           sig=(n == 5))
                z.free = t_G = cp(AC, G[:, c, :], z.ap[:, 0:256], t)
            rk = sb([128, 64, 2], F32, sc)
            t = ts(PO, rk[:], mvc[:, :, :, 1], 1e-5, None, ALU.add, None)
            for b in range(0, 64, 32):
                t_rk = tt(PO, rk[:, b:b + 32, :], rk[:, b:b + 32, :], negh[:].rearrange("p (b k) -> p b k", k=2),
                          ALU.pow, t)
            mt = sb([64, 9], F32, sc)
            tT = sb([128, 2, 64], F32, sc)
            t = DV.do(lambda e: e.bn_stats(mt[:, 0:6], tailc[:]), tw)
            t = DV.do(lambda e: e.bn_aggr(mt[:, 6:8], mt[:, 0:6]), t)
            t = ts(PO, mt[:, 8:9], mt[:, 7:8], 1e-5, None, ALU.add, None, t)
            t = tt(PO, mt[:, 8:9], mt[:, 8:9], negh[0:64, 0:1], ALU.pow, t)
            t_tail = ts(DV, tailc[:], tailc[:], mt[:, 6:7], mt[:, 8:9], ALU.subtract, ALU.mult, t)
            l_t = Landing(sem("l_t"))
            t_tail = SP.dma(l_t, A["scratch"], tailc[:], t_tail)
            z = slots.next()
            for c in range(2):
                t = tr(z.ap[:, c * 64:(c + 1) * 64], tailc[:, c * 128:(c + 1) * 128], ident[0:64, 0:64], z.free,
                       (DV.sem, DV.n), sig=(c == 1))
            for c in range(2):
                z.free = t_tT = ts(DV, tT[:, c, :], z.ap[:, c * 64:(c + 1) * 64], col("L2_xattn_tab_g", c),
                                   col("L2_xattn_tab_b", c), ALU.mult, ALU.add, t)

            ptl = sb([128, 2, 64], F32, sc)
            rt = sb([1, 64], F32, sc)
            z = slots.next()
            for m in range(2):
                for c in range(2):
                    t = mm(z.ap[:, m * 64:(m + 1) * 64], G[:, c, m * 128:(m + 1) * 128], tT[:, c, :], c == 0, c == 1,
                           t_tT, t_G, z.free, sig=(c == 1 and m == 1))
            z.free = t = tt(DV, ptl[:], z.ap[:, 0:128].rearrange("p (m s) -> p m s", m=2), tT[:], ALU.mult, t)
            z = slots.next()
            for m in range(2):
                t = mm(z.ap[0:1, 0:64], ones[:, 0:1], ptl[:, m, :], m == 0, m == 1, t, z.free, sig=(m == 1))
            z.free = t = ts(DV, rt[:], z.ap[0:1, 0:64], 1.0 / 768, 1e-5, ALU.mult, ALU.add, t)
            t_rt = tt(PO, rt[:], rt[:], negh[0:1, :], ALU.pow, t)

            qn = sb([128, 768], F32, sc)
            qT = sb([128, 6, 128], F32, sc)
            qk = sb([128, 6, 128], F32, sc)
            stq = sb([128, 2, 6], F32, sc)
            mq = sb([128, 4], F32, sc)
            Qp = [sb([128, 2, 4, 384], F32, sc) for _ in range(2)]
            rbt = [sb([128, 12], F32, sc) for _ in range(2)]
            rb = sb([128, 64, 3], F32, sc)
            cn = [sb([128, 2, 256], F32, sc) for _ in range(7)]
            cr = [sb([1, 256], F32, sc) for _ in range(8)]
            kvT = [sb([128, 2, 257], F32, sc) for _ in range(4)]
            wf = wk[:].rearrange("p c m -> p (c m)")
            pr = [wf[:, 512 * k:512 * (k + 1)].rearrange("p (m s) -> p m s", m=2) for k in range(2)]
            dg = [wf[:, 1024 + 256 * k:1280 + 256 * k].rearrange("p (t s) -> p t s", t=2) for k in range(2)]
            vk = sb([128, 64, 2], F32, sc)
            rv = [sb([128, 257], F32, sc) for _ in range(2)]
            flat = xn[:].rearrange("p i d -> p (i d)")
            S = [flat[:, 771 * k:771 * (k + 1)].rearrange("p (n s) -> p n s", n=3) for k in range(2)]
            PT = [flat[:, 1542 + 768 * k:1542 + 768 * (k + 1)].rearrange("p (t n) -> p t n", t=2) for k in range(2)]
            Pt = [sb([1, 384], F32, sc) for _ in range(2)]
            sm = sb([128, 2, 5, 3], F32, sc)
            Pc = [sb([128, 2, 12, 128], F32, sc) for _ in range(2)]
            oT = sb([128, 6, 128], F32, sc)
            B = {}
            l_r = [Landing(sem(f"l_r{k}")) for k in range(8)]

            def qa(i):
                zz = [slots.next(), slots.next()]
                for n in range(2):
                    for c in range(2):
                        t = mm(zz[n].ap[:, 0:384], xT[:, c, i * 128:(i + 1) * 128], wq[:, c, n * 384:(n + 1) * 384],
                               c == 0, c == 1, zz[n].free, out[i // 4], tw, sig=(c == 1))
                for n in range(2):
                    t1 = DV.do(lambda e, n=n: e.bn_stats(stq[:, n, :], zz[n].ap[:, 0:384]), t)
                t1 = DV.do(lambda e: e.bn_aggr(mq[:, 0:2], stq[:].rearrange("p a b -> p (a b)")), t1)
                t1 = ts(PO, mq[:, 2:3], mq[:, 1:2], 1e-5, None, ALU.add, None, t1)
                t1 = tt(PO, mq[:, 2:3], mq[:, 2:3], negh[:, 0:1], ALU.pow, t1)
                for n in range(2):
                    zz[n].free = B["qn", i] = ts(DV, qn[:, n * 384:(n + 1) * 384], zz[n].ap[:, 0:384], mq[:, 0:1],
                                                 mq[:, 2:3], ALU.subtract, ALU.mult, t1, was(B, "qt", i - 1))

            def qb(i):
                tk = []
                for n in range(2):
                    z = slots.next()
                    for v in range(3):
                        t = tr(z.ap[:, v * 128:(v + 1) * 128], qn[:, (3 * n + v) * 128:(3 * n + v + 1) * 128], ident[:],
                               B["qn", i], z.free, sig=(v == 2))
                    for v in range(3):
                        ch = 3 * n + v
                        z.free = ts(DV, qT[:, ch, :], z.ap[:, v * 128:(v + 1) * 128], col("L2_xattn_q_g", ch),
                                    col("L2_xattn_q_b", ch), ALU.mult, ALU.add, t, was(B, "qp", i - 1))
                        tk.append(z.free)
                B["qt", i] = t
                B["qT", i] = tk
                B["qk", i] = tt(PO, qk[:], qT[:], cbc("L2_xattn_k_g", 0, 6, 128), ALU.mult, tk, was(B, "qp", i - 1))

            def qc(i):
                k = i % 2
                z = slots.next()
                for ch in range(6):
                    t = mm(z.ap[:, 0:12], qT[:, ch, :], kb[:, ch, :], ch == 0, ch == 5, B["qT", i], tw, z.free, sig=(ch == 5))
                z.free = B["rbt", i] = cp(AC, rbt[k][:], z.ap[:, 0:12], t, was(B, "rb", 4 * i - 5))
                for m in range(2):
                    for par in range(2):
                        for hf in range(2):
                            z = slots.next()
                            for v in range(3):
                                ch = 3 * hf + v
                                t = mm(z.ap[:, v * 128:(v + 1) * 128], wkT[64 * par:64 * par + 64, ch, m * 128:(m + 1) * 128],
                                       qk[64 * par:64 * par + 64, ch, :], True, True, B["qk", i], z.free, sig=(v == 2))
                            d = Qp[k][:, m, :, :].rearrange("p j (c a q) -> p j c a q", a=2, q=32)[:, :, 3 * hf:3 * hf + 3, par, :]
                            z.free = cp(AC if par else DV, d, z.ap[:, 0:384].rearrange("p (c j q) -> p j c q", c=3, j=4), t,
                                        was(B, "sc", 4 * i - 5))
                            B["Qp", i, m, par, hf] = z.free
                B["qp", i] = t
                B["Qp", i] = [B["Qp", i, m, par, hf] for m in range(2) for par in range(2) for hf in range(2)]

            def c0(b):
                s = ring.next()
                s.full = SP.dma(s.land, s.ap[0][:], A["ctx"][b, 0:256, :].rearrange("(k p) d -> p k d", p=128), s.free)
                B["r", b] = SP.dma(l_r[b % 8], cr[b % 8][:], A["scratch"][b:b + 1, :], t_tail, was(B, "pc", b - 8))
                B[b] = s
                if b % 4 == 0:
                    qa(b // 4)
                if b % 4 == 1:
                    qb(b // 4)
                if b % 4 == 2:
                    qc(b // 4)

            def c1(b):
                s = B[b]
                for kt in range(2):
                    t = ts(PO, cn[b % 7][:, kt, :], s.ap[0][:, kt, :], mvc[:, b, kt, 0:1], rk[:, b, kt:kt + 1],
                           ALU.subtract, ALU.mult, s.full, t_rk, was(B, "pc", b - 7))
                s.free = t
                B["cn", b] = t

            def c2(b):
                z = slots.next()
                for c in range(2):
                    for kt in range(2):
                        t = tr(z.ap[:, c * 256 + kt * 128:c * 256 + (kt + 1) * 128],
                               cn[b % 7][:, kt, c * 128:(c + 1) * 128], ident[:], B["cn", b], z.free, sig=(c == 1 and kt == 1))
                tk = []
                for c in range(2):
                    z.free = ts(DV, kvT[b % 4][:, c, 0:256], z.ap[:, c * 256:(c + 1) * 256], col("L2_xattn_tab_g", c),
                                col("L2_xattn_tab_b", c), ALU.mult, ALU.add, t, was(B, "sc", b - 4))
                    tk.append(z.free)
                tk.append(cp(PO, kvT[b % 4][:, :, 256:257], tT[:, :, b:b + 1], t_tT, was(B, "sc", b - 4)))
                B["kvT", b] = tk

            def c3(b):
                z = slots.next()
                for m in range(2):
                    for c in range(2):
                        t = mm(z.ap[:, m * 256:(m + 1) * 256], G[:, c, m * 128:(m + 1) * 128], kvT[b % 4][:, c, 0:256],
                               c == 0, c == 1, B["kvT", b], t_G, z.free, sig=(c == 1 and m == 1))
                z.free = B["pr", b] = tt(DV, pr[b % 2], z.ap[:].rearrange("p (m s) -> p m s", m=2),
                                         kvT[b % 4][:, :, 0:256], ALU.mult, t, was(B, "v", b - 2))

            def c4(b):
                z = slots.next()
                for kt in range(2):
                    for m in range(2):
                        t = mm(z.ap[:, kt:kt + 1], pr[b % 2][:, m, kt * 128:(kt + 1) * 128], ones[:, 0:1], m == 0, m == 1,
                               B["pr", b], z.free, sig=(m == 1 and kt == 1))
                B["v", b] = t
                z.free = t = ts(DV, vk[:, b, :], z.ap[:, 0:2], 1.0 / 768, 1e-5, ALU.mult, ALU.add, t)
                t = tt(PO, vk[:, b, :], vk[:, b, :], negh[:, 0:2], ALU.pow, t)
                for kt in range(2):
                    t2 = ts(PO, dg[b % 2][:, kt, :], ident[:], vk[:, b, kt:kt + 1], None, ALU.mult, None, t,
                            was(B, "rvp", b - 2))
                B["dg", b] = t2

            def c4b(b):
                z = slots.next()
                for kt in range(2):
                    mm(z.ap[:, kt * 128:(kt + 1) * 128], ones[:], dg[b % 2][:, kt, :], True, True, B["dg", b], z.free)
                B["rvp", b] = t = mm(z.ap[:, 256:257], ones[0:1, :], rt[:, b:b + 1], True, True, t_rt, sig=True)
                z.free = B["rv", b] = cp(AC, rv[b % 2][:], z.ap[:, 0:257], t, was(B, "S", b - 2))

            def c5(b):
                i, j = b // 4, b % 4
                k = b % 2
                m = lambda n: sm[:, k, n, :]
                tk = []
                for n in range(3):
                    z = slots.next()
                    for c in range(2):
                        t = mm(z.ap[:, 0:257], Qp[i % 2][:, c, j, n * 128:(n + 1) * 128], kvT[b % 4][:, c, :],
                               c == 0, c == 1, B["Qp", i], z.free, sig=(c == 1))
                    B["sc", b] = t
                    z.free = ttr(S[k][:, n, :], z.ap[:, 0:257], rv[k][:], ALU.mult, ALU.max, -3.4e38, m(0)[:, n:n + 1],
                                 t, B["rv", b], was(B, "T", b - 2))
                    tk.append(z.free)
                B["S", b] = tk
                rv_ = rbt[i % 2][:].rearrange("p (n h) -> p n h", h=4)
                for h in range(4):
                    t2 = cp(AC, rb[32 * h:32 * h + 32, b, :], rv_[32 * j:32 * j + 32, :, h], B["rbt", i])
                B["rb", b] = t2
                t = tt(DV, m(1), m(0), rb[:, b, :], ALU.add, tk, t2)
                t = tt(DV, m(2), rb[:, b, :], m(1), ALU.subtract, t)
                t = ts(DV, m(2), m(2), 0.125, None, ALU.mult, None, t)
                te = []
                for n in range(3):
                    te.append(act(S[k][:, n, :], S[k][:, n, :], ACT.Exp, t, bias=m(2)[:, n:n + 1], scale=0.125,
                                  acc=m(3)[:, n:n + 1]))
                t = recip(m(4), m(3), te)
                for n in range(3):
                    t = ts(DV, S[k][:, n, :], S[k][:, n, :], m(4)[:, n:n + 1], None, ALU.mult, None,
                           t if n == 0 else None)
                B["P", b] = t

            def c6(b):
                k = b % 2
                for kt in range(3):
                    z = slots.next()
                    for n in range(3):
                        if kt < 2:
                            t = tr(z.ap[:, n * 128:(n + 1) * 128], S[k][:, n, kt * 128:(kt + 1) * 128], ident[:], B["P", b],
                                   z.free, sig=(n == 2))
                        else:
                            t = tr(z.ap[0:1, n * 128:(n + 1) * 128], S[k][:, n, 256:257], ident[:], z.free, sig=(n == 2))
                    if kt < 2:
                        z.free = cp(AC, PT[k][:, kt, :], z.ap[:, 0:384], t, was(B, "pc", b - 2))
                    else:
                        z.free = cp(AC, Pt[k][:], z.ap[0:1, 0:384], t, was(B, "pc", b - 2))
                B["T", b] = t
                B["PT", b] = z.free

            def c7(b):
                i, j, k = b // 4, b % 4, b % 2
                tk = []
                for m in range(2):
                    z = slots.next()
                    for kt in range(2):
                        mm(z.ap[:, 0:384], cn[b % 7][:, kt, m * 128:(m + 1) * 128], PT[k][:, kt, :], kt == 0, False,
                           B["PT", b], z.free)
                    t = mm(z.ap[:, 0:384], cr[b % 8][:, m * 128:(m + 1) * 128], Pt[k][:], False, True, B["r", b], sig=True)
                    z.free = act(Pc[i % 2][:, m, :, 32 * j:32 * j + 32], z.ap[:, 0:384].rearrange("p (h q) -> p h q", q=32),
                                 ACT.Identity, t, was(B, "o", i - 2), bias=col("L2_xattn_tab_b", m),
                                 scale=col("L2_xattn_tab_g", m))
                    tk.append(z.free)
                B["pc", b] = t
                B["Pc", b] = tk

            def c8(b):
                if b % 4 < 3:
                    return
                i = b // 4
                zz = [slots.next(), slots.next()]
                w_ = [B["Pc", 4 * i + n] for n in range(4)]
                for ch in range(6):
                    for par in range(2):
                        h = 2 * ch + par
                        for m in range(2):
                            t = mm(zz[ch // 3].ap[64 * par:64 * par + 64, (ch % 3) * 128:(ch % 3 + 1) * 128],
                                   wv[:, m, h * 64:(h + 1) * 64], Pc[i % 2][:, m, h, :], m == 0, m == 1, w_,
                                   zz[ch // 3].free, sig=(m == 1 and par == 1 and ch % 3 == 2))
                    if ch % 3 == 2:
                        B["oz", i, ch // 3] = t
                B["o", i] = t
                for n in range(2):
                    zz[n].free = cp([AC, DV][n], oT[:, 3 * n:3 * n + 3, :], zz[n].ap[:, 0:384].rearrange("p (c t) -> p c t", c=3),
                                    B["oz", i, n], was(B, "x", i - 1))
                B["oT", i] = [zz[0].free, zz[1].free]

            def c9(b):
                if b % 4 < 3:
                    return
                i = b // 4
                z = slots.next()
                mm(z.ap[:, 0:256], ones[0:1, :], bo[:], True, False, z.free, t_ones, tw)
                for ch in range(6):
                    t = mm(z.ap[:, 0:256], oT[:, ch, :], wo[:, ch, :], False, ch == 5, B["oT", i], sig=(ch == 5))
                B["x", i] = t
                z.free = add_x(i, z.ap[:, 0:256], t)

            pipeline(64, [c0, c1, c2, c3, c4, c4b, c5, c6, c7, c8, c9])

    def l2_attn(par):
        with ExitStack() as sc:
            take = loader(sc, par)
            wq, _ = take(A["L2a_q"], split=1)
            wk, _ = take(A["L2a_k"], split=1)
            wv, _ = take(A["L2a_v"], split=1)
            wo, _ = take(A["L2a_o"], split=4)
            T = lambda shape: sb(shape, F32, sc)
            keep, bias, nk, nv = T([128, 32]), T([128, 16, 34]), T([32, 128]), T([32, 8, 128])
            SP.dma(l_w[par], keep[:], A["keep8"])
            SP.dma(l_w[par], bias[:], A["alibi"])
            SP.dma(l_w[par], nk[:], A["L2a_nk"])
            tw = SP.dma(l_w[par], nv[:], A["L2a_nv"])
            for q in (DV, PO, PE):
                q.wait(tw)
            xT2 = T([128, 2, 2048])
            out, out2 = layernorm(second=(1e-5, False, col("L2_attn_norm_g"), col("L2_attn_norm_b")), keep=xT2)
            ring = Ring([Slot(bank[6]), Slot(bank[7])])
            nn = T([32, 4])
            nkT = T([128, 8, 4])
            sqn = T([32, 128])
            t = act(sqn[:], nk[:], ACT.Square, tw, acc=nn[:, 0:1])
            t = ts(PO, nn[:, 1:2], nn[:, 0:1], 1e-24, None, ALU.max, None, t)
            t = tt(PO, nn[:, 2:3], nn[:, 1:2], negh[0:32, 0:1], ALU.pow, t)
            t = ts(DV, nk[:], nk[:], nn[:, 2:3], None, ALU.mult, None, t)
            z = ring.next()
            t = tr(z.ap[:, 0:32], nk[:], ident[0:32, 0:32], t, z.free, sig=True)
            z.free = t_nk = ts(DV, nkT[:].rearrange("p c n -> p (c n)"), z.ap[:, 0:32], col("L2_attn_k_scale", 0), None,
                               ALU.mult, None, t, t_cols)
            sq = [T([128, 512]) for _ in range(2)]
            ss = T([128, 4, 8])
            qn = [T([128, 2, 1024]) for _ in range(1)]
            qT = [T([128, 8, 128]) for _ in range(2)]
            kT = [T([128, 8, 128]) for _ in range(2)]
            v = [T([128, 1024]) for _ in range(5)]
            B, ready = {}, {}

            def p1(i):
                for n in range(4):
                    z = ring.next()
                    src, w, o = ((xT, wq, out), (xT2, wk, out2))[n // 2]
                    for c in range(2):
                        t = mm(z.ap[:], src[:, c, i * 128:(i + 1) * 128], w[:, c, (n % 2) * 512:(n % 2 + 1) * 512],
                               c == 0, c == 1, z.free, o[i // 4], tw, sig=(c == 1))
                    key = 4 * i + n
                    t3 = act(sq[n % 2][:], z.ap[:], ACT.Square, t, was(B, "ss", key - 2))
                    t3 = red(ss[:, n, :], sq[n % 2][:].rearrange("p (h d) -> p h d", d=64), ALU.add, t3)
                    B["ss", key] = t3
                    t3 = ts(PO, ss[:, n, :], ss[:, n, :], 1e-24, None, ALU.max, None, t3)
                    t3 = tt(PO, ss[:, n, :], ss[:, n, :], negh[:, 0:8], ALU.pow, t3)
                    z.free = B["qn", key] = tt(DV, qn[0][:, n // 2, (n % 2) * 512:(n % 2 + 1) * 512].rearrange("p (h d) -> p h d", d=64),
                                               z.ap[:].rearrange("p (h d) -> p h d", d=64),
                                               ss[:, n, :].unsqueeze(2).to_broadcast([128, 8, 64]), ALU.mult, t3,
                                               was(B, "tr", i - 1))
                tk = []
                for hf in range(2):
                    z = ring.next()
                    for c in range(2):
                        t = mm(z.ap[:], xT2[:, c, i * 128:(i + 1) * 128], wv[:, c, hf * 512:(hf + 1) * 512], c == 0,
                               c == 1, z.free, sig=(c == 1))
                    z.free = cp(AC, v[i % 5][:, hf * 512:(hf + 1) * 512], z.ap[:], t)
                    tk.append(z.free)
                B["v", i] = tk

            def p2(i):
                tk = []
                for n in range(4):
                    z = ring.next()
                    for c in range(4):
                        t = tr(z.ap[:, c * 128:(c + 1) * 128],
                               qn[0][:, n // 2, ((n % 2) * 4 + c) * 128:((n % 2) * 4 + c + 1) * 128], ident[:],
                               B["qn", 4 * i + n], z.free, sig=(c == 3))
                    dst = (qT, kT)[n // 2][i % 2][:, (n % 2) * 4:(n % 2) * 4 + 4, :].rearrange("p c t -> p (c t)")
                    nw = ("L2_attn_q_scale", "L2_attn_k_scale")[n // 2]
                    if n % 2:
                        z.free = act(dst, z.ap[:], ACT.Copy, t, t_cols, scale=col(nw, 0))
                    else:
                        z.free = ts(DV, dst, z.ap[:], col(nw, 0), None, ALU.mult, None, t, t_cols)
                    tk.append(z.free)
                B["tr", i] = t
                ready[i] = (qT[i % 2], kT[i % 2], v[i % 5], tk + B["v", i])

            self_attention(sc, [p1, p2], 64, ready, wo, tw, scale=1.0, keep=keep, bias=bias,
                           null=(nkT, nv, t_nk, 8.0), ring=ring)

    def l2_ffn(par):
        with ExitStack() as sc:
            T = lambda shape: sb(shape, F32, sc)
            take = loader(sc, par)
            w1, _ = take(A["L2f_1"], split=1)
            w2, tw = take(A["L2f_2"], split=1)
            lh = [Landing(sem("l_n1")), Landing(sem("l_n2")), Landing(sem("l_n3"))]
            h1, h2, w3, s3 = T([128, 8, 1024]), T([128, 8, 1024]), T([128, 8, 256]), T([128, 256])
            for c in range(8):
                th1 = SP.dma(lh[0], h1[:, c, :], A["L2f_h1"][c * 128:(c + 1) * 128, :])
            for c in range(8):
                th2 = SP.dma(lh[1], h2[:, c, :], A["L2f_h2"][c * 128:(c + 1) * 128, :])
            SP.dma(lh[2], w3[:], A["L2f_3"].rearrange("(c p) m -> p c m", p=128))
            th3 = SP.dma(lh[2], s3[:], A["L2_ffn_w3_s"].rearrange("(a n) -> a n", a=1).to_broadcast([128, 256]))
            out, _ = layernorm()
            slots = Ring([Slot(b) for b in bank])
            H = Ring([Slot(T([128, 8, 512])) for _ in range(3)])
            tmp = Ring([Slot(T([128, 512])) for _ in range(2)])
            B = {}

            def f1(g):
                h = H.next()
                tk = []
                for m in range(8):
                    z1, z2 = slots.next(), slots.next()
                    for z, w in ((z1, w1), (z2, w2)):
                        for c in range(2):
                            t = mm(z.ap[:], w[:, c, m * 128:(m + 1) * 128], xT[:, c, g * 512:(g + 1) * 512], c == 0, c == 1,
                                   z.free, out[g], tw, sig=(c == 1))
                    u = tmp.next()
                    z1.free = t1 = act(u.ap[:], z1.ap[:], ACT.Silu, t, u.free, t_cols, scale=col("L2_ffn_w1_s", m))
                    z2.free = u.free = stt(h.ap[:, m, :], z2.ap[:], col("L2_ffn_w2_s", m), u.ap[:], ALU.mult, ALU.mult,
                                           t1, t, h.free)
                    tk.append(u.free)
                B["h", 0, g] = (h, tk)

            def mid(n, w, tww, sname):
                def f(g):
                    src, tk0 = B["h", n, g]
                    h = H.next()
                    tk = []
                    for m in range(8):
                        z = slots.next()
                        for c in range(8):
                            t = mm(z.ap[:], w[:, c, m * 128:(m + 1) * 128], src.ap[:, c, :], c == 0, c == 7, z.free, tww,
                                   tk0, sig=(c == 7))
                        z.free = act(h.ap[:, m, :], z.ap[:], ACT.Gelu, t, t_cols, h.free, scale=col(sname, m))
                        tk.append(z.free)
                    src.free = t
                    B["h", n + 1, g] = (h, tk)
                return f

            def f4(g):
                src, tk0 = B["h", 2, g]
                for k in range(4):
                    z = slots.next()
                    i = 4 * g + k
                    for c in range(8):
                        t = mm(z.ap[:, 0:256], src.ap[:, c, k * 128:(k + 1) * 128], w3[:, c, :], c == 0, c == 7, z.free,
                               th3, tk0, sig=(c == 7))
                    u = tmp.next()
                    z.free = t1 = tt(DV, u.ap[:, 0:256], z.ap[:, 0:256], s3[:], ALU.mult, t, u.free)
                    u.free = add_x(i, u.ap[:, 0:256], t1)
                src.free = t

            for g in range(4):
                f1(g)
                mid(0, h1, th1, "L2_ffn_h1_s")(g)
                mid(1, h2, th2, "L2_ffn_h2_s")(g)
                f4(g)

    def l3_xattn(par):
        with ExitStack() as sc:
            T = lambda shape: sb(shape, F32, sc)
            take = loader(sc, par)
            wq, _ = take(A["L3x_q"])
            wk, _ = take(A["L3x_k"])
            wv, _ = take(A["L3x_v"])
            wo, _ = take(A["L3x_o"])
            bo, _ = rows(sc, par, "L3_xattn_bo")
            hm = T([128, 8])
            tw = SP.dma(l_w[par], hm[:], A["headmask"])
            DV.wait(tw)
            ring = Ring([Slot(T([128, 2, 257]), Landing(sem(f"l_l{k}"))) for k in range(4)])
            out, _ = layernorm()
            slots = Ring([Slot(b) for b in bank])
            qT = T([128, 2, 2048])
            tq = {}
            for g in range(4):
                tq[g] = project_T(slots, wq, xT, qT, "L3_xattn_bq", g, tw, out[g])
            QX = [T([128, 2, 8, 32]) for _ in range(3)]
            kT = [T([128, 2, 257]) for _ in range(2)]
            V = [T([128, 2, 256]) for _ in range(5)]
            Vt = [T([1, 256]) for _ in range(5)]
            S = [T([128, 4, 257]) for _ in range(2)]
            PT = [T([128, 2, 512]) for _ in range(2)]
            Pt = [T([1, 512]) for _ in range(2)]
            sm = T([128, 2, 3, 4])
            ot = [T([128, 256]) for _ in range(2)]
            oT = [T([128, 2, 128]) for _ in range(2)]
            B = {}

            def f0(b):
                s = ring.next()
                s.full = SP.dma(s.land, s.ap[:], A["ctxT"][b].rearrange("(c p) s -> p c s", p=128), s.free)
                B[b] = s

            def f1(b):
                s = B[b]
                tk = []
                for m in range(2):
                    tk.append(tt(PO, QX[b % 3][:, m], qT[:, m, 32 * b:32 * b + 32].unsqueeze(1).to_broadcast([128, 8, 32]),
                                 hm[:].unsqueeze(2).to_broadcast([128, 8, 32]), ALU.mult, tq[b // 16], tw,
                                 was(B, "sc", b - 3)))
                B["QX", b] = tk
                tk = []
                for m in range(2):
                    z = slots.next()
                    for c in range(2):
                        t = mm(z.ap[:, 0:257], wk[:, c, m * 128:(m + 1) * 128], s.ap[:, c, :], c == 0, c == 1, s.full,
                               tw, z.free, sig=(c == 1))
                    z.free = act(kT[b % 2][:, m, :], z.ap[:, 0:257], ACT.Identity, t, t_cols, was(B, "sc", b - 2),
                                 bias=col("L3_xattn_bk", m))
                    tk.append(z.free)
                B["kT", b] = tk
                z = slots.next()
                for kt in range(2):
                    for c in range(2):
                        t = mm(z.ap[:, kt * 256:(kt + 1) * 256], s.ap[:, c, kt * 128:(kt + 1) * 128], wv[:, c, :],
                               c == 0, c == 1, z.free, sig=(c == 1 and kt == 1))
                z.free = t1 = cp(DV, V[b % 5][:], z.ap[:].rearrange("p (k d) -> p k d", k=2), t, was(B, "pv", b - 5))
                z = slots.next()
                for c in range(2):
                    t = mm(z.ap[0:1, 0:256], s.ap[:, c, 256:257], wv[:, c, :], c == 0, c == 1, z.free, sig=(c == 1))
                s.free = t
                z.free = t2 = cp(DV, Vt[b % 5][:], z.ap[0:1, 0:256], t, was(B, "pv", b - 5))
                B["V", b] = [t1, t2]

            def f2(b):
                k = b % 2
                m = lambda n: sm[:, k, n, :]
                tk = []
                for n in range(4):
                    z = slots.next()
                    t = mm(z.ap[:, 0:257], QX[b % 3][:, n // 2, 4 * (n % 2):4 * (n % 2) + 4, :].rearrange("p h q -> p (h q)"),
                           kT[k][:, n // 2, :], True, True, B["QX", b], B["kT", b], z.free, sig=True)
                    t1 = red(m(0)[:, n:n + 1], z.ap[:, 0:257], ALU.max, t, was(B, "pvo", b - 2))
                    t1 = ts(DV, m(1)[:, n:n + 1], m(0)[:, n:n + 1], -0.25, None, ALU.mult, None, t1)
                    z.free = act(S[k][:, n, :], z.ap[:, 0:257], ACT.Exp, t1, was(B, "T", b - 2), bias=m(1)[:, n:n + 1],
                                 scale=0.25, acc=m(2)[:, n:n + 1])
                    tk.append(z.free)
                B["sc", b] = t
                B["P", b] = tk
                B["ri", b] = recip(m(0), m(2), tk)

            def f3(b):
                k = b % 2
                for kt in range(3):
                    z = slots.next()
                    for n in range(4):
                        if kt < 2:
                            t = tr(z.ap[:, n * 128:(n + 1) * 128], S[k][:, n, kt * 128:(kt + 1) * 128], ident[:], B["P", b],
                                   z.free, sig=(n == 3))
                        else:
                            t = tr(z.ap[0:1, n * 128:(n + 1) * 128], S[k][:, n, 256:257], ident[:], z.free, sig=(n == 3))
                    if kt < 2:
                        z.free = cp([AC, DV][kt], PT[k][:, kt, :], z.ap[:], t, was(B, "pv", b - 2))
                        B["PT", b, kt] = z.free
                    else:
                        z.free = cp(AC, Pt[k][:], z.ap[0:1, :], t, was(B, "pv", b - 2))
                B["T", b] = t
                B["PT", b] = [z.free, B["PT", b, 0], B["PT", b, 1]]

            def f4(b):
                k = b % 2
                i, j = b // 4, b % 4
                z = slots.next()
                for n in range(4):
                    o = z.ap[:, n * 64:(n + 1) * 64]
                    for kt in range(2):
                        mm(o, PT[k][:, kt, n * 128:(n + 1) * 128], V[b % 5][:, kt, n * 64:(n + 1) * 64], kt == 0, False,
                           B["PT", b], B["V", b], z.free)
                    t = mm(o, Pt[k][:, n * 128:(n + 1) * 128], Vt[b % 5][:, n * 64:(n + 1) * 64], False, True, sig=(n == 3))
                B["pv", b] = t
                for h in range(4):
                    src = z.ap[32 * h:32 * h + 32, 0:256].rearrange("p (n a) -> p n a", n=4)[:, :, 16 * h:16 * h + 16]
                    dst = ot[i % 2][32 * j:32 * j + 32, :].rearrange("p (n a) -> p n a", n=4)[:, :, 16 * h:16 * h + 16]
                    t2 = tt(DV, dst, src, sm[32 * h:32 * h + 32, k, 0, :].unsqueeze(2).to_broadcast([32, 4, 16]), ALU.mult,
                            t, B["ri", b], was(B, "oX", i - 2))
                z.free = B["pvo", b] = t2

            def f5(b):
                if b % 4 < 3:
                    return
                i = b // 4
                z = slots.next()
                for c in range(2):
                    t = tr(z.ap[:, c * 128:(c + 1) * 128], ot[i % 2][:, c * 128:(c + 1) * 128], ident[:], B["pvo", b],
                           z.free, sig=(c == 1))
                B["oX", i] = t
                for c in range(2):
                    z.free = act(oT[i % 2][:, c, :], z.ap[:, c * 128:(c + 1) * 128], ACT.Identity, t, was(B, "x", i - 2),
                                 bias=col("L3_xattn_bv", c))
                B["oT", i] = z.free

            def f6(b):
                if b % 4 < 3:
                    return
                i = b // 4
                z = slots.next()
                mm(z.ap[:, 0:256], ones[0:1, :], bo[:], True, False, z.free, t_ones, tw)
                for c in range(2):
                    t = mm(z.ap[:, 0:256], oT[i % 2][:, c, :], wo[:, c, :], False, c == 1, B["oT", i], sig=(c == 1))
                B["x", i] = t
                z.free = add_x(i, z.ap[:, 0:256], t)

            pipeline(64, [f0, f1, f2, f3, f4, f5, f6])

    def l3_ffn(par):
        with ExitStack() as sc:
            T = lambda shape, dt=F32: sb(shape, dt, sc)
            MAGIC = 12582912.0
            pk, wi, wb = T([128, 2, 64], I32), T([128, 2, 256], I32), T([128, 2, 256], BF16)
            wsc, bb, bz = T([128, 1]), T([128, 256]), T([128, 256])
            idb = T([128, 128], BF16)
            SP.dma(l_w[par], pk[:], A["packed"].rearrange("(c p) r -> p c r", p=128))
            SP.dma(l_w[par], wsc[:], A["L3_ffn_weight_scale"].rearrange("(a n) -> a n", a=1).to_broadcast([128, 1]))
            tw = SP.dma(l_w[par], bb[:], A["L3_ffn_bias"].rearrange("(a n) -> a n", a=1).to_broadcast([128, 256]))
            t_id = cp(PO, idb[:], ident[:], t_ident)
            for s in range(4):
                t = DV.do(lambda e, s=s: e.tensor_scalar(wi[:, :, 64 * s:64 * s + 64], pk[:], 2 * s, 3,
                                                         ALU.logical_shift_right, ALU.bitwise_and), tw)
            t_wb = ts(DV, wb[:], wi[:], -1.0, None, ALU.add, None, t)
            xq = T([128, 16, 256], BF16)
            am, inv = T([128, 16, 3]), T([128, 16])
            qf = [T([128, 256]) for _ in range(2)]
            xqT = T([128, 2, 2048], BF16)
            B = {}
            slots = Ring([Slot(b) for b in bank])
            PE.wait(DV.now(), AC.now())

            def a(g):
                B["n", g] = normed(xtok, g, x, xn, 1e-5)

            def b_(g):
                tk = apply_norm(B["n", g], g, x, xn)
                for k in range(4):
                    i = 4 * g + k
                    t = DV.do(lambda e, i=i: e.tensor_reduce(am[:, i, 0:1], xn[:, i, :], AX.X, ALU.max,
                                                             apply_absolute_value=True), tk[k])
                    t = ts(DV, am[:, i, 0:1], am[:, i, 0:1], 1e-5, None, ALU.max, None, t)
                    t = recip(am[:, i, 1:2], am[:, i, 0:1], t)
                    t = ts(DV, am[:, i, 1:2], am[:, i, 1:2], 127.0, None, ALU.mult, None, t)
                    t2 = recip(am[:, i, 2:3], am[:, i, 1:2], t)
                    t2 = ts(DV, inv[:, i:i + 1], am[:, i, 2:3], wsc[:], None, ALU.mult, None, t2)
                    t3 = ts(DV, qf[k % 2][:], xn[:, i, :], am[:, i, 1:2], MAGIC, ALU.mult, ALU.add, t, was(B, "q", i - 2))
                    t3 = ts(DV, qf[k % 2][:], qf[k % 2][:], -MAGIC, 127.0, ALU.add, ALU.min, t3)
                    B["q", i] = ts(DV, xq[:, i, :], qf[k % 2][:], -128.0, None, ALU.max, None, t3)
                    B["inv", i] = t2

            def c_(g):
                for c in range(2):
                    z = slots.next()
                    zb = z.ap[:, 0:256].bitcast(BF16)
                    for k in range(4):
                        i = 4 * g + k
                        t = tr(zb[:, k * 128:(k + 1) * 128], xq[:, i, c * 128:(c + 1) * 128], idb[:], B["q", i], t_id,
                               z.free, sig=(k == 3))
                    z.free = cp(AC, xqT[:, c, g * 512:(g + 1) * 512], zb, t)
                B["T", g] = z.free

            def d_(g):
                for k in range(4):
                    i = 4 * g + k
                    z = slots.next()
                    for c in range(2):
                        t = mm(z.ap[:, 0:256], xqT[:, c, i * 128:(i + 1) * 128], wb[:, c, :], c == 0, c == 1, B["T", g],
                               t_wb, z.free, sig=(c == 1))
                    xb = tt(PO, x[:, i, :], x[:, i, :], bb[:], ALU.add, xtok[i], tw, B["inv", i], B["q", i])
                    z.free = xtok[i] = stt(x[:, i, :], z.ap[:, 0:256], inv[:, i:i + 1], x[:, i, :], ALU.mult, ALU.add,
                                           t, xb, B["inv", i])

            pipeline(4, [a, b_, c_, d_])

    def dump(n):
        if dbg is not None:
            l_d = Landing(sem(f"l_d{n}"))
            for g in range(4):
                SP.dma(l_d, dbg[n].rearrange("(i p) d -> p i d", p=128)[:, 4 * g:4 * g + 4, :],
                       x[:, 4 * g:4 * g + 4, :], xtok[4 * g:4 * g + 4])
            for q in compute:
                q.wait((l_d.sem, l_d.n))

    layers = [l0_xattn, l0_attn, l0_ffn, l1_xattn, l1_attn, l1_ffn, l2_xattn, l2_attn, l2_ffn, l3_xattn,
              l3_attn, l3_ffn]
    for n, layer in enumerate(layers[:STAGES]):
        barrier()
        layer(n % 2)
        dump(n)

    for g in range(4):
        SP.dma(l_out, out.rearrange("b s d -> (b s) d").rearrange("(i p) d -> p i d", p=128)[:, 4 * g:4 * g + 4, :],
               x[:, 4 * g:4 * g + 4, :], xtok[4 * g:4 * g + 4])
    SP.wait((l_out.sem, l_out.n))

    block = ctx.enter_context(nc.Block())

    @block.sync
    def _(e):
        SP.emit(e)

    @block.tensor
    def _(e):
        PE.emit(e)

    @block.vector
    def _(e):
        DV.emit(e)

    @block.scalar
    def _(e):
        AC.emit(e)

    @block.gpsimd
    def _(e):
        PO.emit(e)


def lerp():
    f = np.float32
    pos = np.clip((np.arange(32, dtype=f) + f(0.5)) * f(257 / 32) - f(0.5), f(0), f(256))
    lo = np.floor(pos).astype(np.int32)
    return lo, np.minimum(lo + 1, 256), pos - lo.astype(f)


def constants():
    c = {}
    d = 64
    timescale = (np.float32(10000.0) ** (np.float32(2.0 / d) * np.arange(d // 2, dtype=np.float32))).astype(np.float32)

    def table(pos):
        rad = (pos.astype(np.float32)[:, None] / timescale).astype(np.float32).astype(np.float64)
        co, si = np.cos(rad), np.sin(rad)
        return np.stack([np.concatenate([co, co], 1), np.concatenate([-si, si], 1)], 0)

    q = table(257 + np.arange(128) % 32) * 0.125
    c["rope_q"] = np.tile(q[:, :, None, :], (1, 1, 4, 1)).reshape(2, 128, 256).transpose(1, 0, 2)
    k = table(np.arange(257))
    c["rope_k"] = k[:, 0:256].reshape(2, 2, 128, 64).transpose(2, 0, 1, 3)
    c["rope_t"] = np.tile(k[:, 256:257].transpose(1, 0, 2), (64, 1, 1))
    w = lerp()[2][np.arange(128) % 32]
    c["lerp"] = np.stack([1 - w, w], 1)
    c["headmask"] = np.arange(128)[:, None] // 16 == np.arange(8)[None, :]
    p, k32 = np.arange(128)[:, None] % 32, np.arange(32)[None, :]
    c["keep"] = (k32 <= p) / 8.0
    c["keep8"] = (k32 <= p) * 8.0
    start = 2.0 ** (-2.0 ** (-(np.log2(16) - 3)))
    slopes = np.array([start * start ** h for h in range(16)], dtype=np.float32)
    head = np.array([2 * ch + par for par in range(2) for ch in range(8)])
    dist = np.abs(np.arange(34)[None, :] - (p + 2))
    c["alibi"] = np.where((np.arange(34)[None, :] > p + 2)[:, None, :], -FMAX,
                          -slopes[head][None, :, None] * dist[:, None, :].astype(np.float32))
    c["neg"] = np.where(k32 <= p, 0.0, -100000.0)
    return {n: np.ascontiguousarray(v.astype(np.float32)) for n, v in c.items()}


def column_block(I, name, c):
    a = I[name]
    if name in ("L0_attn_qn_w", "L0_attn_kn_w"):
        a = np.tile(np.concatenate([a, np.zeros(16, a.dtype)]), 4)
    if name in ("L2_attn_q_scale", "L2_attn_k_scale"):
        a = np.tile(a, 2)
    if name == "L1_ffn_b_up":
        a = np.concatenate([a, np.zeros((4, 86), a.dtype)], axis=1)
    return a.reshape(c, 128).T


def layout(I):
    L = {}
    L["x"] = I["x"]
    L["ctx"] = I["ctx_1024"]
    L["ctxT"] = I["ctx_1024"].transpose(0, 2, 1)
    L["tailT"] = I["ctx_1024"][:, 256, :].T
    L["mask"] = I["mask_BxS2_bk0"].reshape(-1).view(np.int32)
    L["cols"] = np.concatenate([column_block(I, n, c) for n, c in COLS], axis=1)
    L["L0x_q"] = I["L0_xattn_q_w"].transpose(1, 0, 2).reshape(256, 256)
    L["L0x_kv"] = I["L0_xattn_kv_w"][:, 0].transpose(1, 0, 2).reshape(256, 128)
    pad = lambda w: np.concatenate([w, np.zeros_like(w)], axis=1)
    L["L0a_qk"] = np.concatenate([I["L0_attn_Wq"].T, I["L0_attn_Wk"].T], axis=1)
    L["L0a_v"] = I["L0_attn_Wv"].T
    L["L0a_o"] = pad(I["L0_attn_Wo"].T.reshape(16, 16, 256)).reshape(512, 256)
    L["L0f_g"], L["L0f_1"], L["L0f_2"] = I["L0_ffn_Wg"], I["L0_ffn_W1"], I["L0_ffn_W2"]
    for k in "QKV":
        L["L1a_" + k.lower()] = I[f"L1_attn_{k}_w"].transpose(1, 0, 2).reshape(256, 1024)
    L["L1a_o"] = I["L1_attn_O_w"].reshape(1024, 256)
    L["L1_attn_O_b"] = I["L1_attn_O_b"]
    L["L1f_r"], L["L1_ffn_br"] = I["L1_ffn_Wr"], I["L1_ffn_br"]
    L["L1f_up"], L["L1f_down"], L["L1_ffn_b_down"] = I["L1_ffn_W_up"], I["L1_ffn_W_down"], I["L1_ffn_b_down"]
    for k in "qkv":
        L["L3a_" + k] = I[f"L3_attn_W{k}"].T
    L["L3a_o"], L["L3_attn_bo"] = I["L3_attn_Wo"].T, I["L3_attn_bo"]
    for k in ("Wq_c", "Wv_s", "Wk_c", "Wv_c", "Wg"):
        L["L1x_" + k[1:].replace("_", "")] = I["L1_xattn_" + k].T
    for k in ("Wk_s", "Wq_s"):
        L["L1x_" + k[1:].replace("_", "")] = I["L1_xattn_" + k]
    lo, hi, _ = lerp()
    L["selT"] = I["ctx_1024"][:, np.concatenate([lo, hi]), :].transpose(2, 0, 1)
    L["L2x_q"], L["L2x_k"], L["L2x_v"] = I["L2_xattn_Wq"], I["L2_xattn_Wk"], I["L2_xattn_Wv"]
    L["L2x_o"], L["L2_xattn_bo"] = I["L2_xattn_Wo"], I["L2_xattn_bo"]
    kb = np.zeros((12, 64, 12), np.float32)
    kb[np.arange(12), :, np.arange(12)] = I["L2_xattn_k_b"].reshape(12, 64)
    L["L2x_kb"] = kb.reshape(768, 12)
    L["L2a_q"], L["L2a_o"] = I["L2_attn_Wq"], I["L2_attn_Wout"]
    L["L2a_k"], L["L2a_v"] = I["L2_attn_Wkv"][:, 0:1024], I["L2_attn_Wkv"][:, 1024:2048]
    null = I["L2_attn_null_kv"].reshape(8, 2, 2, 2, 64)
    nk = np.zeros((8, 2, 2, 2, 64), np.float32)
    nv = np.zeros((2, 8, 2, 8, 2, 64), np.float32)
    for par in range(2):
        nk[:, par, :, par, :] = null[:, par, :, 0, :]
        for ch in range(8):
            nv[par, ch, :, ch, par, :] = null[ch, par, :, 1, :]
    L["L2a_nk"], L["L2a_nv"] = nk.reshape(32, 128), nv.reshape(32, 8, 128)
    L["L2f_1"], L["L2f_2"], L["L2f_3"] = I["L2_ffn_w1_w"].T, I["L2_ffn_w2_w"].T, I["L2_ffn_w3_w"].T
    L["L2f_h1"], L["L2f_h2"], L["L2_ffn_w3_s"] = I["L2_ffn_h1_w"].T, I["L2_ffn_h2_w"].T, I["L2_ffn_w3_s"]
    for k in "qkvo":
        L["L3x_" + k] = I["L3_xattn_W" + k].T
    L["L3_xattn_bo"] = I["L3_xattn_bo"]
    L["packed"] = I["L3_ffn_packed_weight"].reshape(64, 256).T
    L["L3_ffn_weight_scale"], L["L3_ffn_bias"] = I["L3_ffn_weight_scale"], I["L3_ffn_bias"]
    L["L0x_o"] = I["L0_xattn_out_w"].reshape(256, 256)
    return L


def kernel(**inputs):
    import concourse.bacc as bacc
    from concourse.bass_utils import run_bass_kernel_spmd

    I = {k: np.asarray(v) for k, v in inputs.items()}
    arrays = {**layout(I), **constants()}
    arrays = {k: np.ascontiguousarray(v) for k, v in arrays.items()}
    nc = bacc.Bacc("TRN2", target_bir_lowering=False, num_devices=1)
    A = {n: nc.dram_tensor(n, a.shape, mybir.dt.from_np(a.dtype), kind="ExternalInput").ap()
         for n, a in arrays.items()}
    out = nc.dram_tensor("out", (64, 32, 256), F32, kind="ExternalOutput").ap()
    dbg = nc.dram_tensor("dbg", (STAGES, 2048, 256), F32, kind="ExternalOutput").ap() if DEBUG else None
    A["scratch"] = nc.dram_tensor("scratch", (64, 256), F32, kind="Internal").ap()
    program(nc, A, out, dbg)
    r = run_bass_kernel_spmd(nc, [arrays], core_ids=[0])
    if DEBUG:
        return tuple(r.results[0]["dbg"][i].reshape(64, 32, 256) for i in range(STAGES))
    return r.results[0]["out"]
```
